# Optimizing a Trainium2 kernel written in Bass

```python
import numpy as np
import jax
import jax.numpy as jnp

def _softmax(x, axis=-1):
    return jax.nn.softmax(x, axis=axis)

def _gelu(x):
    return jax.nn.gelu(x, approximate=True)

def _silu(x):
    return jax.nn.silu(x)

def _sigmoid(x):
    return jax.nn.sigmoid(x)

def _layernorm(x, axis=-1, eps=1e-05):
    m = jnp.mean(x, axis=axis, keepdims=True)
    v = jnp.var(x, axis=axis, keepdims=True)
    return (x - m) / jnp.sqrt(v + eps)

def _scatter_add(tgt, idx, src, axis=0):
    return tgt.at[idx].add(src)

def _segment_sum(src, seg, n):
    return jax.ops.segment_sum(src, seg, n)
kernel_name = 'mk_xattn_ffn_d1_seqx_r2_90cb10'

def setup_inputs(seed: int=0):
    np.random.seed(seed)
    _w = jnp.asarray

    def _rec_inputs():
        import jax
        import jax.numpy as jnp
        _rk = jax.random.key(seed)
        x = 7.22e-05 + 1 * jax.random.normal(jax.random.fold_in(_rk, 1), (2, 2048, 512), jnp.float32)
        _lenS = 2048 - jax.random.randint(jax.random.fold_in(_rk, 7), (2,), 0, max(1, 2048 // 4) + 1, jnp.int32)
        _lenS2 = 77 - jax.random.randint(jax.random.fold_in(_rk, 8), (2,), 0, max(1, 77 // 4) + 1, jnp.int32)
        _ctx_1024P = jax.random.normal(jax.random.fold_in(_rk, 11), (2, 16, 512), jnp.float32)
        _ctx_1024c = jax.random.dirichlet(jax.random.fold_in(_rk, 511), 0.3 * jnp.ones((16,), jnp.float32), (2, 77))
        _ctx_1024t = jnp.einsum('bsk,bkd->bsd', _ctx_1024c, _ctx_1024P)
        _ctx_1024t = _ctx_1024t * jax.lax.rsqrt(jnp.mean(jnp.square(_ctx_1024t)) + 1e-12) * 0.953939
        ctx_1024 = 2.81802e-05 + 1.00001 * (_ctx_1024t + 0.3 * jax.random.normal(jax.random.fold_in(_rk, 611), (2, 77, 512), jnp.float32))
        _validS = jnp.arange(2048)[None, :] < _lenS[:, None]
        _validS2 = jnp.arange(77)[None, :] < _lenS2[:, None]
        _causal = jnp.tril(jnp.ones((2048, 2048), dtype=bool))
        mask_BxS2_bk0 = jnp.logical_not(jnp.broadcast_to(_validS2[:, :], (2, 77)))
        return (x, ctx_1024, mask_BxS2_bk0)
    x, ctx_1024, mask_BxS2_bk0 = _rec_inputs()

    def _L0_xattn_setup():
        import jax, jax.numpy as jnp
        import numpy as np
        B, LQ, LKV = (8, 512, 1024)
        QDIM, KDIM, HID = (512, 512, 512)
        key = jax.random.key(seed)
        ks = jax.random.split(key, 12)
        s = lambda d: 1.0 / np.sqrt(d)
        return {'query': jax.random.normal(ks[0], (B, LQ, QDIM), jnp.float32), 'key_value': jax.random.normal(ks[1], (B, LKV, KDIM), jnp.float32), 'key_mask': jax.random.randint(ks[2], (B, LKV), 0, 2).astype(bool), 'Wq': jax.random.uniform(ks[3], (QDIM, HID), jnp.float32, -s(QDIM), s(QDIM)), 'bq': jax.random.uniform(ks[4], (HID,), jnp.float32, -s(QDIM), s(QDIM)), 'Wk': jax.random.uniform(ks[5], (KDIM, HID), jnp.float32, -s(KDIM), s(KDIM)), 'bk': jax.random.uniform(ks[6], (HID,), jnp.float32, -s(KDIM), s(KDIM)), 'Wv': jax.random.uniform(ks[7], (KDIM, HID), jnp.float32, -s(KDIM), s(KDIM)), 'bv': jax.random.uniform(ks[8], (HID,), jnp.float32, -s(KDIM), s(KDIM)), 'Wo': jax.random.uniform(ks[9], (HID, QDIM), jnp.float32, -s(HID), s(HID)), 'bo': jax.random.uniform(ks[10], (QDIM,), jnp.float32, -s(HID), s(HID))}
    _L0_xattn_all = _L0_xattn_setup()
    _L0_xattn_in = {k: v for k, v in _L0_xattn_all.items() if k in ('Wq', 'bq', 'Wk', 'bk', 'Wv', 'bv', 'Wo', 'bo')}
    del _L0_xattn_all

    def _L0_ffn_setup():
        import jax, jax.numpy as jnp
        import numpy as np
        INPUT_SIZE = 512
        OUTPUT_SIZE = 512
        key = jax.random.key(seed)
        kx, kt, kp, ktn, kpn = jax.random.split(key, 5)
        x = jax.random.normal(kx, (8, 1024, INPUT_SIZE), dtype=jnp.float32)
        theta = jax.random.normal(kt, (INPUT_SIZE, OUTPUT_SIZE), dtype=jnp.float32) * 0.02
        phi = jax.random.normal(kp, (INPUT_SIZE, OUTPUT_SIZE), dtype=jnp.float32) * 0.02
        theta_noise = jax.random.normal(ktn, (INPUT_SIZE, OUTPUT_SIZE), dtype=jnp.float32) * 0.01
        phi_noise = jax.random.normal(kpn, (INPUT_SIZE, OUTPUT_SIZE), dtype=jnp.float32) * 0.01
        return {'x': x, 'theta': theta, 'phi': phi, 'theta_noise': theta_noise, 'phi_noise': phi_noise}
    _L0_ffn_all = _L0_ffn_setup()
    _L0_ffn_in = {k: v for k, v in _L0_ffn_all.items() if k in ('theta', 'phi', 'theta_noise', 'phi_noise')}
    del _L0_ffn_all
    return {'x': x, 'ctx_1024': ctx_1024, 'mask_BxS2_bk0': mask_BxS2_bk0, 'L0_xattn_Wq': _L0_xattn_in['Wq'], 'L0_xattn_bq': _L0_xattn_in['bq'], 'L0_xattn_Wk': _L0_xattn_in['Wk'], 'L0_xattn_bk': _L0_xattn_in['bk'], 'L0_xattn_Wv': _L0_xattn_in['Wv'], 'L0_xattn_bv': _L0_xattn_in['bv'], 'L0_xattn_Wo': _L0_xattn_in['Wo'], 'L0_xattn_bo': _L0_xattn_in['bo'], 'L0_ffn_theta': _L0_ffn_in['theta'], 'L0_ffn_phi': _L0_ffn_in['phi'], 'L0_ffn_theta_noise': _L0_ffn_in['theta_noise'], 'L0_ffn_phi_noise': _L0_ffn_in['phi_noise']}

def reference(x, ctx_1024, mask_BxS2_bk0, L0_xattn_Wq, L0_xattn_bq, L0_xattn_Wk, L0_xattn_bk, L0_xattn_Wv, L0_xattn_bv, L0_xattn_Wo, L0_xattn_bo, L0_ffn_theta, L0_ffn_phi, L0_ffn_theta_noise, L0_ffn_phi_noise):
    import jax
    import jax.numpy as jnp

    def _L0_xattn_ref(query, key_value, key_mask, Wq, bq, Wk, bk, Wv, bv, Wo, bo):
        import jax, jax.numpy as jnp
        import numpy as np
        B, LQ, LKV = (8, 512, 1024)
        QDIM, KDIM, HID = (512, 512, 512)
        Q = query @ Wq + bq
        K = key_value @ Wk + bk
        V = key_value @ Wv + bv
        hid = Q.shape[-1]
        scores = jnp.einsum('bqh,bkh->bqk', Q, K) / jnp.sqrt(jnp.float32(hid))
        scores = jnp.where(key_mask[:, None, :], scores, jnp.float32(-1000000000.0))
        attn = jax.nn.softmax(scores, axis=-1)
        context = jnp.einsum('bqk,bkh->bqh', attn, V)
        return context @ Wo + bo

    def _L0_ffn_ref(x, theta, phi, theta_noise, phi_noise):
        import jax, jax.numpy as jnp
        import numpy as np
        INPUT_SIZE = 512
        OUTPUT_SIZE = 512
        real = jnp.einsum('bti,io->bto', x, jnp.cos(theta + theta_noise))
        imag = jnp.einsum('bti,io->bto', x, jnp.sin(phi + phi_noise))
        return jnp.sqrt(real * real + imag * imag)
    x = x + _L0_xattn_ref(_layernorm(x, axis=-1), ctx_1024, mask_BxS2_bk0, L0_xattn_Wq, L0_xattn_bq, L0_xattn_Wk, L0_xattn_bk, L0_xattn_Wv, L0_xattn_bv, L0_xattn_Wo, L0_xattn_bo)
    x = x + _L0_ffn_ref(_layernorm(x, axis=-1), L0_ffn_theta, L0_ffn_phi, L0_ffn_theta_noise, L0_ffn_phi_noise)
    return x

_drawn_inputs = setup_inputs


def setup_inputs(seed=0):
    import zlib

    import numpy as np

    out = dict(_drawn_inputs(seed))
    spreads = {}
    factors = {'L0_xattn_bq': 45.396,
     'L0_xattn_bk': 64.0,
     'L0_xattn_bv': 3.979,
     'L0_ffn_theta': 8.0,
     'L0_ffn_theta_noise': 8.0}
    for name, (base, spread) in spreads.items():
        noise = np.random.default_rng([zlib.crc32(name.encode()), seed]).standard_normal(out[name].shape)
        drawn = base * np.exp(spread * noise) if base else spread * noise
        out[name] = jnp.asarray(drawn.astype(out[name].dtype))
    for name, factor in factors.items():
        out[name] = (out[name] * factor).astype(out[name].dtype)
    return out
```

```python
import math
from contextlib import ExitStack

import numpy as np

import concourse.bass as bass
from concourse import mybir

F32 = mybir.dt.float32
F16 = mybir.dt.float16
U8 = mybir.dt.uint8
ALU = mybir.AluOpType
ACT = mybir.ActivationFunctionType
AX = mybir.AxisListType

P = 128
BATCH, SEQ, DIM, KEYS = 2, 2048, 512, 77
HID = DIM
CH = DIM // P
TILES = 4
ROWS = TILES * P
GROUPS = BATCH * SEQ // ROWS
BLOCKS = GROUPS // BATCH
KK = BATCH * KEYS
LN_EPS = 1e-5
MASKED = 1e9
SM_SCALE = 1.0 / math.sqrt(HID)
H_SCALE = 256.0
W_SCALE = 4096.0
UNSCALE = 1.0 / (H_SCALE * W_SCALE)
ROUND = 1.5 * 2.0 ** 23
TURN_HI = 6.28125
TURN_LO = 2.0 * math.pi - TURN_HI
SIN_MAX = 3.1415925


def build(nc, x, xT, ctxT, mask, Wk, WqT, Wv, Wo, bq, bk, bv, bo, theta, theta_noise, phi, phi_noise, out):
    with ExitStack() as ctx:
        def sb(name, shape, dt=F32):
            return ctx.enter_context(nc.sbuf_tensor(name, shape, dt))

        def bank(name):
            return ctx.enter_context(nc.psum_tensor(name, [P, DIM], F32))

        def sem(name):
            return ctx.enter_context(nc.semaphore(name))

        wk = sb("wk", [P, CH, HID])
        wqT = sb("wqT", [P, CH, DIM])
        wv = sb("wv", [P, CH, HID])
        wo = sb("wo", [P, CH, DIM])
        ctx_t = sb("ctx_t", [P, CH, KK])
        mask8 = sb("mask8", [P, KK], U8)
        bias_q = sb("bias_q", [P, CH])
        bias_k = sb("bias_k", [P, CH])
        bias_v = sb("bias_v", [P, CH])
        bo_rows = sb("bo_rows", [KEYS, DIM])
        angle_w = [sb(f"angle_w{i}", [P, CH * DIM]) for i in range(2)]
        angle_n = [sb(f"angle_n{i}", [P, CH * DIM]) for i in range(2)]
        turns = sb("turns", [P, CH * DIM])

        ones_mean = sb("ones_mean", [P, P])
        bq_cols = sb("bq_cols", [P, CH, P])
        kT = sb("kT", [P, CH, KK])
        vT = sb("vT", [P, CH, KK])
        a_raw = sb("a_raw", [P, CH, KK])
        a_mid = sb("a_mid", [P, CH, KK])
        a_keys = sb("a_keys", [P, CH, KK])
        keep = sb("keep", [P, KK])
        keep_off = sb("keep_off", [P, KK])
        c_mid = sb("c_mid", [P, KK])
        c_keys = sb("c_keys", [P, KK])
        vw = sb("vw", [KEYS, BATCH, DIM])
        w_hi = [sb(f"w_hi{i}", [P, CH, DIM], F16) for i in range(2)]
        w_lo = [sb(f"w_lo{i}", [P, CH, DIM], F16) for i in range(2)]
        ident = sb("ident", [P, P])
        minus_half = sb("minus_half", [P, TILES])
        eps = sb("eps", [P, TILES])

        xb = [sb(f"xb{i}", [P, TILES, DIM]) for i in range(2)]
        xTb = sb("xTb", [P, CH, ROWS])
        stats1 = sb("stats1", [P, TILES, 6])
        mv1 = sb("mv1", [P, TILES, 2])
        veps1 = sb("veps1", [P, TILES])
        rstd1 = sb("rstd1", [P, TILES])
        logits = sb("logits", [P, TILES, KEYS])
        shifted = sb("shifted", [P, TILES, KEYS])
        top = sb("top", [P, TILES])
        probs = sb("probs", [P, TILES, KEYS])
        total = sb("total", [P, TILES])
        inv_total = sb("inv_total", [P, TILES])
        probsT = sb("probsT", [KEYS, ROWS])
        x2 = [sb(f"x2_{i}", [P, TILES, DIM]) for i in range(2)]
        stats2 = sb("stats2", [P, TILES, 6])
        mv2 = sb("mv2", [P, TILES, 2])
        veps2 = sb("veps2", [P, TILES])
        rstd2 = sb("rstd2", [P, TILES])
        h = [sb(f"h{i}", [P, DIM]) for i in range(2)]
        hT_hi = [sb(f"hT_hi{j}", [P, CH, P], F16) for j in range(TILES)]
        hT_lo = [sb(f"hT_lo{j}", [P, CH, P], F16) for j in range(TILES)]
        sq_re = [sb(f"sq_re{i}", [P, DIM]) for i in range(2)]
        sq_im = [sb(f"sq_im{i}", [P, DIM]) for i in range(2)]
        power = sb("power", [P, TILES, DIM])
        root = sb("root", [P, TILES, DIM])
        result = sb("result", [P, TILES, DIM])

        re_bank = [bank("re0"), bank("re1")]
        im_bank = [bank("im0"), bank("im1")]
        score_bank = bank("score_bank")
        pT_bank = bank("pT_bank")
        att_bank = bank("att_bank")
        hT_bank = bank("hT_bank")
        prep = [re_bank[0], re_bank[1], im_bank[0], im_bank[1], score_bank, pT_bank, att_bank, hT_bank]

        ld_ctx, ld_wk, ld_wq, ld_wv, ld_wo = (sem(f"ld_{n}") for n in ("ctx", "wk", "wq", "wv", "wo"))
        ld_bq, ld_bk, ld_bv, ld_bo, ld_mask = (sem(f"ld_{n}") for n in ("bq", "bk", "bv", "bo", "mask"))
        ld_angle = [sem("ld_theta"), sem("ld_phi")]
        consts_made = sem("consts_made")
        v_consts = sem("v_consts")
        kT_mm, kT_ready = sem("kT_mm"), sem("kT_ready")
        a_mm, a_copied = sem("a_mm"), sem("a_copied")
        c_mm, mean_mm = sem("c_mm"), sem("mean_mm")
        a_centred, keys_ready = sem("a_centred"), sem("keys_ready")
        vT_mm, vT_ready = sem("vT_mm"), sem("vT_ready")
        vw_mm, vw_ready = sem("vw_mm"), sem("vw_ready")
        angle_step = sem("angle_step")
        angle_ready = sem("angle_ready")
        sine_made = sem("sine_made")
        w_hi_ready, w_ready = sem("w_hi_ready"), sem("w_ready")
        x_loaded = [sem("x_loaded0"), sem("x_loaded1")]
        xT_loaded, stored = sem("xT_loaded"), sem("stored")
        stats1_made, mean1_made, eps1_added, rstd1_made = (sem(f"{n}") for n in ("stats1_made", "mean1_made", "eps1_added", "rstd1_made"))
        scores_mm, scores_read, top_found, shifted_made = (sem(f"{n}") for n in ("scores_mm", "scores_read", "top_found", "shifted_made"))
        probs_made, total_made, inv_total_made = sem("probs_made"), sem("total_made"), sem("inv_total_made")
        pT_mm, pT_copied = sem("pT_mm"), sem("pT_copied")
        att_mm, x2_made = sem("att_mm"), sem("x2_made")
        stats2_made, mean2_made, eps2_added, rstd2_made = (sem(f"{n}") for n in ("stats2_made", "mean2_made", "eps2_added", "rstd2_made"))
        h_made, hT_mm, hi_made, lo_made = sem("h_made"), sem("hT_mm"), sem("hi_made"), sem("lo_made")
        re_mm, im_mm, re_squared, im_squared, power_made = (sem(f"{n}") for n in ("re_mm", "im_mm", "re_squared", "im_squared", "power_made"))
        root_made, result_made = sem("root_made"), sem("result_made")

        LAST = GROUPS - 1

        block = ctx.enter_context(nc.Block())

        @block.sync
        def _(sp):
            def load_x(batch, blk):
                sp.dma_start(xb[batch][:, :, :], x[batch, blk]).then_inc(x_loaded[batch], 16)

            def load_xT(batch, blk):
                sp.dma_start(xTb[:, :, :], xT[batch, blk]).then_inc(xT_loaded, 16)

            sp.dma_start(ctx_t[:, :, :], ctxT).then_inc(ld_ctx, 16)
            sp.dma_start(wk[:, :, :], Wk).then_inc(ld_wk, 16)
            sp.dma_start(bias_k[:, :], bk).then_inc(ld_bk, 16)
            sp.dma_start(angle_w[0][:, :], theta).then_inc(ld_angle[0], 16)
            sp.dma_start(angle_n[0][:, :], theta_noise).then_inc(ld_angle[0], 16)
            sp.dma_start(bias_q[:, :], bq).then_inc(ld_bq, 16)
            sp.dma_start(mask8[:, :], mask).then_inc(ld_mask, 16)
            sp.dma_start(wqT[:, :, :], WqT).then_inc(ld_wq, 16)
            load_xT(0, 0)
            load_x(0, 0)
            sp.dma_start(bias_v[:, :], bv).then_inc(ld_bv, 16)
            sp.dma_start(bo_rows[:, :], bo).then_inc(ld_bo, 16)
            sp.dma_start(wv[:, :, :], Wv).then_inc(ld_wv, 16)
            sp.dma_start(wo[:, :, :], Wo).then_inc(ld_wo, 16)
            sp.dma_start(angle_w[1][:, :], phi).then_inc(ld_angle[1], 16)
            sp.dma_start(angle_n[1][:, :], phi_noise).then_inc(ld_angle[1], 16)
            load_x(1, 0)
            sp.wait_ge(scores_mm, 1)
            load_xT(1, 0)

            def step(n, batch, blk, load, store):
                if load:
                    sp.wait_ge(x2_made, TILES * (n + 1))
                    load_x(batch, blk)
                    sp.wait_ge(scores_mm, n + 2)
                    load_xT(batch, blk)
                if store:
                    sp.wait_ge(result_made, n)
                    sp.dma_start(out[1 - batch, blk - 1 - (1 - batch)], result[:, :, :]).then_inc(stored, 16)

            step(0, 0, 1, True, False)
            with sp.Fori(0, 2) as i:
                step(2 * i + 1, 1, i + 1, True, True)
                step(2 * i + 2, 0, i + 2, True, True)
            step(5, 1, 3, True, True)
            step(6, 0, 4, False, True)
            step(7, 1, 4, False, True)
            for j in range(TILES):
                sp.wait_ge(result_made, LAST + j + 1)
                sp.dma_start(out[1, BLOCKS - 1, :, j, :], result[:, j, :]).then_inc(stored, 16)
            sp.wait_ge(stored, 16 * (LAST + TILES))

        @block.gpsimd
        def _(pool):
            nc.gpsimd.memset(minus_half[:, :], -0.5)
            nc.gpsimd.memset(eps[:, :], LN_EPS)
            nc.gpsimd.memset(ident[:, :], 0.0).then_inc(consts_made, 1)
            pool.wait_ge(consts_made, 1)
            nc.gpsimd.affine_select(out=ident[:, :], in_=ident[:, :], compare_op=ALU.not_equal, fill=1.0,
                                    base=0, pattern=[[-1, P]], channel_multiplier=1).then_inc(consts_made, 1)

            def rstd_of_x(m):
                pool.wait_ge(mean1_made, m + 1)
                nc.gpsimd.tensor_tensor(veps1[:, :], mv1[:, :, 1], eps[:, :], ALU.add).then_inc(eps1_added, 1)
                pool.wait_ge(eps1_added, m + 1)
                nc.gpsimd.tensor_tensor(rstd1[:, :], veps1[:, :], minus_half[:, :], ALU.pow).then_inc(rstd1_made, 1)

            def rstd_of_x2(m, j):
                pool.wait_ge(mean2_made, TILES * m + j + 1)
                nc.gpsimd.tensor_tensor(veps2[:, j:j + 1], mv2[:, j, 1:2], eps[:, 0:1], ALU.add).then_inc(eps2_added, 1)
                pool.wait_ge(eps2_added, TILES * m + j + 1)
                nc.gpsimd.tensor_tensor(rstd2[:, j:j + 1], veps2[:, j:j + 1], minus_half[:, 0:1], ALU.pow).then_inc(rstd2_made, 1)

            def step(m):
                rstd_of_x(m)
                for j in range(TILES):
                    rstd_of_x2(m, j)

            step(0)
            step(1)
            with pool.Fori(0, 3) as i:
                step(2 * i + 2)
                step(2 * i + 3)

        @block.tensor
        def _(pe):
            pe.wait_ge(ld_ctx, 16)
            pe.wait_ge(ld_wk, 16)
            for c in range(CH):
                for k in range(CH):
                    last = nc.tensor.matmul(prep[c][:, 0:KK], wk[:, k, P * c:P * c + P], ctx_t[:, k, :],
                                            start=(k == 0), stop=(k == CH - 1))
                last.then_inc(kT_mm, 1)
            pe.wait_ge(ld_wq, 16)
            pe.wait_ge(kT_ready, CH)
            for c in range(CH):
                for k in range(CH):
                    last = nc.tensor.matmul(prep[4 + c][:, 0:KK], wqT[:, k, P * c:P * c + P], kT[:, k, :],
                                            start=(k == 0), stop=(k == CH - 1))
                last.then_inc(a_mm, 1)
            pe.wait_ge(v_consts, 3)
            for k in range(CH):
                last = nc.tensor.matmul(prep[0][:, 0:KK], bq_cols[:, k, :], kT[:, k, :],
                                        start=(k == 0), stop=(k == CH - 1))
            last.then_inc(c_mm, 1)
            pe.wait_ge(a_copied, CH)
            for k in range(CH):
                last = nc.tensor.matmul(prep[1][:, 0:KK], ones_mean[:, :], a_raw[:, k, :],
                                        start=(k == 0), stop=(k == CH - 1))
            last.then_inc(mean_mm, 1)

            def scores(m, batch):
                pe.wait_ge(xT_loaded, 16 * (m + 1))
                if not isinstance(m, int) or m > 0:
                    pe.wait_ge(scores_read, m)
                for j in range(TILES):
                    for k in range(CH):
                        last = nc.tensor.matmul(score_bank[:, KEYS * j:KEYS * j + KEYS], xTb[:, k, P * j:P * j + P],
                                                a_keys[:, k, KEYS * batch:KEYS * batch + KEYS],
                                                start=(k == 0), stop=(k == CH - 1))
                last.then_inc(scores_mm, 1)

            def transpose_probs(m):
                pe.wait_ge(probs_made, m + 1)
                if not isinstance(m, int) or m > 0:
                    pe.wait_ge(pT_copied, m)
                for j in range(TILES):
                    last = nc.tensor.transpose(pT_bank[0:KEYS, P * j:P * j + P], probs[:, j, :], ident[:, :])
                last.then_inc(pT_mm, 1)

            def attend(m, batch, j):
                pe.wait_ge(pT_copied, m + 1)
                if j or not isinstance(m, int) or m > 0:
                    pe.wait_ge(x2_made, TILES * m + j)
                nc.tensor.matmul(att_bank[:, :], probsT[:, P * j:P * j + P], vw[:, batch, :],
                                 start=True, stop=True).then_inc(att_mm, 1)

            def transpose_h(m, j):
                pe.wait_ge(h_made, TILES * m + j + 1)
                if j or not isinstance(m, int) or m > 0:
                    pe.wait_ge(lo_made, TILES * m + j)
                for k in range(CH):
                    last = nc.tensor.transpose(hT_bank[:, P * k:P * k + P], h[j % 2][:, P * k:P * k + P], ident[:, :])
                last.then_inc(hT_mm, 1)

            def feed(n, j, part):
                bank_ = (re_bank, im_bank)[part][j % 2]
                pe.wait_ge(lo_made, TILES * n + j + 1)
                if j >= 2 or not isinstance(n, int) or n > 0:
                    pe.wait_ge((re_squared, im_squared)[part], TILES * n + j - 1)
                for k in range(CH):
                    nc.tensor.matmul(bank_[:, :], hT_hi[j][:, k, :], w_hi[part][:, k, :], start=(k == 0), stop=False)
                    nc.tensor.matmul(bank_[:, :], hT_hi[j][:, k, :], w_lo[part][:, k, :], start=False, stop=False)
                    last = nc.tensor.matmul(bank_[:, :], hT_lo[j][:, k, :], w_hi[part][:, k, :],
                                            start=False, stop=(k == CH - 1))
                last.then_inc((re_mm, im_mm)[part], 1)

            pe.wait_ge(keys_ready, 2)
            scores(0, 0)
            pe.wait_ge(ld_wv, 16)
            for c in range(CH):
                bank_ = prep[2 + c] if c < 2 else prep[3 + c]
                for k in range(CH):
                    last = nc.tensor.matmul(bank_[:, 0:KK], wv[:, k, P * c:P * c + P], ctx_t[:, k, :],
                                            start=(k == 0), stop=(k == CH - 1))
                last.then_inc(vT_mm, 1)
            pe.wait_ge(ld_wo, 16)
            pe.wait_ge(vT_ready, CH)
            pe.wait_ge(keys_ready, 2)
            for b in range(BATCH):
                for k in range(CH):
                    last = nc.tensor.matmul(prep[b][0:KEYS, :], vT[:, k, KEYS * b:KEYS * b + KEYS], wo[:, k, :],
                                            start=(k == 0), stop=(k == CH - 1))
                last.then_inc(vw_mm, 1)
            pe.wait_ge(consts_made, 2)
            transpose_probs(0)
            pe.wait_ge(vw_ready, BATCH)
            attend(0, 0, 0)
            attend(0, 0, 1)
            attend(0, 0, 2)
            transpose_h(0, 0)
            attend(0, 0, 3)
            transpose_h(0, 1)
            transpose_h(0, 2)

            def step(n, batch):
                scores(n + 1, batch)
                transpose_h(n, 3)
                feed(n, 0, 0)
                feed(n, 0, 1)
                transpose_probs(n + 1)
                feed(n, 1, 0)
                attend(n + 1, batch, 0)
                feed(n, 1, 1)
                attend(n + 1, batch, 1)
                feed(n, 2, 0)
                attend(n + 1, batch, 2)
                feed(n, 2, 1)
                attend(n + 1, batch, 3)
                transpose_h(n + 1, 0)
                feed(n, 3, 0)
                transpose_h(n + 1, 1)
                feed(n, 3, 1)
                transpose_h(n + 1, 2)

            scores(1, 1)
            transpose_h(0, 3)
            pe.wait_ge(w_ready, 2)
            feed(0, 0, 0)
            feed(0, 0, 1)
            transpose_probs(1)
            feed(0, 1, 0)
            attend(1, 1, 0)
            feed(0, 1, 1)
            attend(1, 1, 1)
            feed(0, 2, 0)
            attend(1, 1, 2)
            feed(0, 2, 1)
            attend(1, 1, 3)
            transpose_h(1, 0)
            feed(0, 3, 0)
            transpose_h(1, 1)
            feed(0, 3, 1)
            transpose_h(1, 2)
            with pe.Fori(0, 3) as i:
                step(2 * i + 1, 0)
                step(2 * i + 2, 1)
            transpose_h(LAST, 3)
            for j in range(TILES):
                feed(LAST, j, 0)
                feed(LAST, j, 1)

        @block.scalar
        def _(act):
            act.wait_ge(ld_bk, 16)
            for c in range(CH):
                act.wait_ge(kT_mm, c + 1)
                nc.scalar.activation(kT[:, c, :], prep[c][:, 0:KK], ACT.Identity,
                                     bias=bias_k[:, c:c + 1]).then_inc(kT_ready, 1)
            for c in range(CH):
                act.wait_ge(a_mm, c + 1)
                nc.scalar.activation(a_raw[:, c, :], prep[4 + c][:, 0:KK], ACT.Copy, scale=SM_SCALE).then_inc(a_copied, 1)

            def sine(part):
                act.wait_ge(angle_ready, part + 1)
                nc.scalar.activation(angle_n[part][:, :], angle_w[part][:, :], ACT.Sin).then_inc(sine_made, 1)
                act.wait_ge(sine_made, part + 1)
                nc.scalar.activation(w_hi[part][:, :, :], angle_n[part][:, :].rearrange("p (c d) -> p c d", c=CH),
                                     ACT.Copy, scale=W_SCALE).then_inc(w_hi_ready, 1)

            def exps(m):
                act.wait_ge(shifted_made, m + 1)
                if not isinstance(m, int) or m > 0:
                    act.wait_ge(pT_mm, m)
                    act.wait_ge(total_made, m)
                nc.scalar.activation(probs[:, :, :], shifted[:, :, :], ACT.Exp).then_inc(probs_made, 1)

            def copy_pT(m):
                act.wait_ge(pT_mm, m + 1)
                if not isinstance(m, int) or m > 0:
                    act.wait_ge(att_mm, TILES * m)
                nc.scalar.activation(probsT[:, :], pT_bank[0:KEYS, :], ACT.Copy).then_inc(pT_copied, 1)

            def high_half(m, j):
                act.wait_ge(hT_mm, TILES * m + j + 1)
                if not isinstance(m, int) or m > 0:
                    act.wait_ge(im_mm, TILES * (m - 1) + j + 1)
                nc.scalar.activation(hT_hi[j][:, :, :], hT_bank[:, :].rearrange("p (c r) -> p c r", c=CH),
                                     ACT.Copy, scale=H_SCALE).then_inc(hi_made, 1)

            def square(n, j, part):
                act.wait_ge((re_mm, im_mm)[part], TILES * n + j + 1)
                if j >= 2 or not isinstance(n, int) or n > 0:
                    act.wait_ge(power_made, TILES * n + j - 1)
                nc.scalar.activation((sq_re, sq_im)[part][j % 2][:, :], (re_bank, im_bank)[part][j % 2][:, :],
                                     ACT.Square, scale=UNSCALE).then_inc((re_squared, im_squared)[part], 1)

            def roots(n):
                act.wait_ge(power_made, TILES * (n + 1))
                if not isinstance(n, int) or n > 0:
                    act.wait_ge(result_made, n)
                nc.scalar.activation(root[:, :, :], power[:, :, :], ACT.Sqrt).then_inc(root_made, 1)

            sine(0)
            exps(0)
            act.wait_ge(ld_bv, 16)
            for c in range(CH):
                bank_ = prep[2 + c] if c < 2 else prep[3 + c]
                act.wait_ge(vT_mm, c + 1)
                nc.scalar.activation(vT[:, c, :], bank_[:, 0:KK], ACT.Identity,
                                     bias=bias_v[:, c:c + 1]).then_inc(vT_ready, 1)
            sine(1)
            copy_pT(0)
            high_half(0, 0)
            high_half(0, 1)

            def step(n, first):
                if not first:
                    square(n - 1, 3, 1)
                high_half(n, 2)
                if not first:
                    roots(n - 1)
                high_half(n, 3)
                exps(n + 1)
                square(n, 0, 0)
                square(n, 0, 1)
                copy_pT(n + 1)
                square(n, 1, 0)
                square(n, 1, 1)
                square(n, 2, 0)
                square(n, 2, 1)
                high_half(n + 1, 0)
                square(n, 3, 0)
                high_half(n + 1, 1)

            step(0, True)
            with act.Fori(0, 3) as i:
                step(2 * i + 1, False)
                step(2 * i + 2, False)
            square(LAST - 1, 3, 1)
            high_half(LAST, 2)
            roots(LAST - 1)
            high_half(LAST, 3)
            for j in range(TILES):
                square(LAST, j, 0)
                square(LAST, j, 1)
                act.wait_ge(power_made, TILES * LAST + j + 1)
                act.wait_ge(result_made, LAST)
                nc.scalar.activation(root[:, j, :], power[:, j, :], ACT.Sqrt).then_inc(root_made, 1)

        @block.vector
        def _(dve):
            nc.vector.memset(ones_mean[:, :], 1.0 / DIM).then_inc(v_consts, 1)
            nc.vector.memset(bq_cols[:, :, :], SM_SCALE).then_inc(v_consts, 1)
            dve.wait_ge(ld_bq, 16)
            dve.wait_ge(v_consts, 2)
            nc.vector.tensor_tensor(bq_cols[:, :, :], bq_cols[:, :, :],
                                    bias_q[:, :].unsqueeze(2).to_broadcast([P, CH, P]), ALU.mult).then_inc(v_consts, 1)
            dve.wait_ge(ld_mask, 16)
            nc.vector.tensor_copy(keep[:, :], mask8[:, :]).then_inc(v_consts, 1)
            dve.wait_ge(v_consts, 4)
            nc.vector.tensor_scalar(keep_off[:, :], keep[:, :], MASKED, -MASKED, ALU.mult, ALU.add).then_inc(v_consts, 1)

            def reduce_angle(part):
                w, noise, k = angle_w[part], angle_n[part], turns
                base = 5 * part
                dve.wait_ge(ld_angle[part], 32)
                nc.vector.scalar_tensor_tensor(out=w[:, :], in0=w[:, :], scalar=(0.5 * math.pi, 0.0)[part],
                                               in1=noise[:, :], op0=ALU.add, op1=ALU.add).then_inc(angle_step, 1)
                dve.wait_ge(angle_step, base + 1)
                nc.vector.tensor_scalar(k[:, :], w[:, :], 1.0 / (2.0 * math.pi), ROUND, ALU.mult, ALU.add).then_inc(angle_step, 1)
                dve.wait_ge(angle_step, base + 2)
                nc.vector.tensor_scalar(k[:, :], k[:, :], ROUND, None, ALU.subtract).then_inc(angle_step, 1)
                dve.wait_ge(angle_step, base + 3)
                nc.vector.scalar_tensor_tensor(out=w[:, :], in0=k[:, :], scalar=-TURN_HI, in1=w[:, :],
                                               op0=ALU.mult, op1=ALU.add).then_inc(angle_step, 1)
                dve.wait_ge(angle_step, base + 4)
                nc.vector.scalar_tensor_tensor(out=w[:, :], in0=k[:, :], scalar=-TURN_LO, in1=w[:, :],
                                               op0=ALU.mult, op1=ALU.add).then_inc(angle_step, 1)
                dve.wait_ge(angle_step, base + 5)
                nc.vector.tensor_scalar(w[:, :], w[:, :], SIN_MAX, -SIN_MAX, ALU.min, ALU.max).then_inc(angle_ready, 1)

            def low_half_of_sine(part):
                dve.wait_ge(w_hi_ready, part + 1)
                nc.vector.scalar_tensor_tensor(
                    out=w_lo[part][:, :, :].rearrange("p c d -> p (c d)"), in0=angle_n[part][:, :], scalar=W_SCALE,
                    in1=w_hi[part][:, :, :].rearrange("p c d -> p (c d)"),
                    op0=ALU.mult, op1=ALU.subtract).then_inc(w_ready, 1)

            def stats_of_x(b, blk):
                dve.wait_ge(x_loaded[b], 16 * (blk + 1))
                for j in range(TILES):
                    last = nc.vector.bn_stats(stats1[:, j, :], xb[b][:, j, :])
                last.then_inc(stats1_made, 1)

            def mean_of_x(m):
                for j in range(TILES):
                    last = nc.vector.bn_aggr(mv1[:, j, :], stats1[:, j, :])
                last.then_inc(mean1_made, 1)

            def softmax_shift(m, b):
                dve.wait_ge(scores_mm, m + 1)
                dve.wait_ge(rstd1_made, m + 1)
                if not isinstance(m, int) or m > 0:
                    dve.wait_ge(shifted_made, m)
                for j in range(TILES):
                    last = nc.vector.scalar_tensor_tensor(
                        out=logits[:, j, :], in0=score_bank[:, KEYS * j:KEYS * j + KEYS], scalar=rstd1[:, j:j + 1],
                        in1=c_keys[:, KEYS * b:KEYS * b + KEYS], op0=ALU.mult, op1=ALU.add)
                last.then_inc(scores_read, 1)
                dve.wait_ge(scores_read, m + 1)
                nc.vector.tensor_reduce(top[:, :], logits[:, :, :], AX.X, ALU.max).then_inc(top_found, 1)
                dve.wait_ge(top_found, m + 1)
                if not isinstance(m, int) or m > 0:
                    dve.wait_ge(probs_made, m)
                nc.vector.tensor_tensor(shifted[:, :, :], logits[:, :, :],
                                        top[:, :].unsqueeze(2).to_broadcast([P, TILES, KEYS]),
                                        ALU.subtract).then_inc(shifted_made, 1)

            def softmax_total(m):
                dve.wait_ge(probs_made, m + 1)
                if not isinstance(m, int) or m > 0:
                    dve.wait_ge(inv_total_made, m)
                nc.vector.tensor_reduce(total[:, :], probs[:, :, :], AX.X, ALU.add).then_inc(total_made, 1)
                dve.wait_ge(total_made, m + 1)
                if not isinstance(m, int) or m > 0:
                    dve.wait_ge(x2_made, TILES * m)
                nc.vector.reciprocal(inv_total[:, :], total[:, :]).then_inc(inv_total_made, 1)

            def residual(m, b, j):
                dve.wait_ge(att_mm, TILES * m + j + 1)
                dve.wait_ge(inv_total_made, m + 1)
                if not isinstance(m, int) or m > 1:
                    dve.wait_ge(result_made, m - 1)
                nc.vector.scalar_tensor_tensor(out=x2[b][:, j, :], in0=att_bank[:, :], scalar=inv_total[:, j:j + 1],
                                               in1=xb[b][:, j, :], op0=ALU.mult, op1=ALU.add).then_inc(x2_made, 1)
                dve.wait_ge(x2_made, TILES * m + j + 1)
                nc.vector.bn_stats(stats2[:, j, :], x2[b][:, j, :]).then_inc(stats2_made, 1)

            def stats_ready(m, j):
                dve.wait_ge(stats2_made, TILES * m + j + 1)

            def mean_of_x2(m, j):
                nc.vector.bn_aggr(mv2[:, j, :], stats2[:, j, :]).then_inc(mean2_made, 1)

            def normalise(m, b, j):
                dve.wait_ge(rstd2_made, TILES * m + j + 1)
                if j >= 2 or not isinstance(m, int) or m > 0:
                    dve.wait_ge(hT_mm, TILES * m + j - 1)
                nc.vector.tensor_scalar(h[j % 2][:, :], x2[b][:, j, :], mv2[:, j, 0:1], rstd2[:, j:j + 1],
                                        ALU.subtract, ALU.mult).then_inc(h_made, 1)

            def low_half(m, j):
                dve.wait_ge(hi_made, TILES * m + j + 1)
                if not isinstance(m, int) or m > 0:
                    dve.wait_ge(im_mm, TILES * (m - 1) + j + 1)
                nc.vector.scalar_tensor_tensor(out=hT_lo[j][:, :, :].rearrange("p c r -> p (c r)"), in0=hT_bank[:, :],
                                               scalar=H_SCALE, in1=hT_hi[j][:, :, :].rearrange("p c r -> p (c r)"),
                                               op0=ALU.mult, op1=ALU.subtract).then_inc(lo_made, 1)

            def add_squares(n, j):
                dve.wait_ge(re_squared, TILES * n + j + 1)
                dve.wait_ge(im_squared, TILES * n + j + 1)
                if not isinstance(n, int) or n > 0:
                    dve.wait_ge(root_made, n)
                nc.vector.tensor_tensor(power[:, j, :], sq_re[j % 2][:, :], sq_im[j % 2][:, :],
                                        ALU.add).then_inc(power_made, 1)

            def finish(n, b):
                dve.wait_ge(root_made, n + 1)
                if not isinstance(n, int) or n > 0:
                    dve.wait_ge(stored, 16 * n)
                nc.vector.tensor_tensor(result[:, :, :], x2[b][:, :, :], root[:, :, :], ALU.add).then_inc(result_made, 1)

            reduce_angle(0)
            dve.wait_ge(mean_mm, 1)
            nc.vector.tensor_tensor(a_mid[:, :, :], a_raw[:, :, :],
                                    prep[1][:, 0:KK].unsqueeze(1).to_broadcast([P, CH, KK]),
                                    ALU.subtract).then_inc(a_centred, 1)
            dve.wait_ge(c_mm, 1)
            nc.vector.tensor_tensor(c_mid[:, :], prep[0][:, 0:KK], keep[:, :], ALU.mult).then_inc(a_centred, 1)
            dve.wait_ge(a_centred, 2)
            nc.vector.tensor_tensor(a_keys[:, :, :], a_mid[:, :, :],
                                    keep[:, :].unsqueeze(1).to_broadcast([P, CH, KK]), ALU.mult).then_inc(keys_ready, 1)
            dve.wait_ge(v_consts, 5)
            nc.vector.tensor_tensor(c_keys[:, :], c_mid[:, :], keep_off[:, :], ALU.add).then_inc(keys_ready, 1)
            dve.wait_ge(keys_ready, 2)
            stats_of_x(0, 0)
            dve.wait_ge(stats1_made, 1)
            mean_of_x(0)
            softmax_shift(0, 0)
            low_half_of_sine(0)
            softmax_total(0)
            reduce_angle(1)
            dve.wait_ge(ld_bo, 16)
            for b in range(BATCH):
                dve.wait_ge(vw_mm, b + 1)
                nc.vector.tensor_tensor(vw[:, b, :], prep[b][0:KEYS, :], bo_rows[:, :], ALU.add).then_inc(vw_ready, 1)
            residual(0, 0, 0)
            stats_ready(0, 0)
            mean_of_x2(0, 0)
            residual(0, 0, 1)
            stats_ready(0, 1)
            normalise(0, 0, 0)
            mean_of_x2(0, 1)
            residual(0, 0, 2)
            stats_ready(0, 2)
            normalise(0, 0, 1)
            mean_of_x2(0, 2)
            low_half(0, 0)
            residual(0, 0, 3)
            stats_ready(0, 3)
            normalise(0, 0, 2)
            mean_of_x2(0, 3)
            low_half(0, 1)
            normalise(0, 0, 3)
            low_half_of_sine(1)

            def step(n, b, blk, first):
                m, a = n + 1, 1 - b
                stats_of_x(a, blk)
                dve.wait_ge(stats1_made, m + 1)
                if not first:
                    add_squares(n - 1, 3)
                mean_of_x(m)
                low_half(n, 2)
                softmax_shift(m, a)
                if not first:
                    finish(n - 1, a)
                low_half(n, 3)
                softmax_total(m)
                add_squares(n, 0)
                residual(m, a, 0)
                stats_ready(m, 0)
                add_squares(n, 1)
                mean_of_x2(m, 0)
                residual(m, a, 1)
                stats_ready(m, 1)
                normalise(m, a, 0)
                mean_of_x2(m, 1)
                residual(m, a, 2)
                stats_ready(m, 2)
                normalise(m, a, 1)
                mean_of_x2(m, 2)
                add_squares(n, 2)
                residual(m, a, 3)
                stats_ready(m, 3)
                normalise(m, a, 2)
                mean_of_x2(m, 3)
                low_half(m, 0)
                normalise(m, a, 3)
                low_half(m, 1)

            step(0, 0, 0, True)
            with dve.Fori(0, 3) as i:
                step(2 * i + 1, 1, i + 1, False)
                step(2 * i + 2, 0, i + 1, False)
            add_squares(LAST - 1, 3)
            low_half(LAST, 2)
            finish(LAST - 1, 0)
            low_half(LAST, 3)
            for j in range(TILES):
                add_squares(LAST, j)
                dve.wait_ge(root_made, LAST + j + 1)
                dve.wait_ge(stored, 16 * LAST)
                nc.vector.tensor_tensor(result[:, j, :], x2[1][:, j, :], root[:, j, :], ALU.add).then_inc(result_made, 1)


def kernel(x, ctx_1024, mask_BxS2_bk0, L0_xattn_Wq, L0_xattn_bq, L0_xattn_Wk, L0_xattn_bk, L0_xattn_Wv, L0_xattn_bv,
           L0_xattn_Wo, L0_xattn_bo, L0_ffn_theta, L0_ffn_phi, L0_ffn_theta_noise, L0_ffn_phi_noise):
    import concourse.bacc as bacc
    from concourse.bass_utils import run_bass_kernel_spmd

    def cols(w):
        w = np.asarray(w)
        return np.ascontiguousarray(w.reshape(CH, P, -1).transpose(1, 0, 2))

    rows = np.asarray(x).reshape(BATCH, BLOCKS, TILES, P, DIM)
    arrays = {
        "x": np.ascontiguousarray(rows.transpose(0, 1, 3, 2, 4)),
        "xT": np.ascontiguousarray(np.asarray(x).reshape(BATCH, BLOCKS, ROWS, CH, P).transpose(0, 1, 4, 3, 2)),
        "ctxT": cols(np.asarray(ctx_1024).reshape(KK, DIM).T),
        "mask": np.ascontiguousarray(np.broadcast_to(np.asarray(mask_BxS2_bk0).reshape(1, KK), (P, KK))),
        "Wk": cols(L0_xattn_Wk),
        "WqT": cols(np.asarray(L0_xattn_Wq).T),
        "Wv": cols(L0_xattn_Wv),
        "Wo": cols(L0_xattn_Wo),
        "bq": np.ascontiguousarray(np.asarray(L0_xattn_bq).reshape(CH, P).T),
        "bk": np.ascontiguousarray(np.asarray(L0_xattn_bk).reshape(CH, P).T),
        "bv": np.ascontiguousarray(np.asarray(L0_xattn_bv).reshape(CH, P).T),
        "bo": np.ascontiguousarray(np.broadcast_to(np.asarray(L0_xattn_bo).reshape(1, DIM), (KEYS, DIM))),
        "theta": cols(L0_ffn_theta).reshape(P, CH * DIM),
        "theta_noise": cols(L0_ffn_theta_noise).reshape(P, CH * DIM),
        "phi": cols(L0_ffn_phi).reshape(P, CH * DIM),
        "phi_noise": cols(L0_ffn_phi_noise).reshape(P, CH * DIM),
    }
    nc = bacc.Bacc("TRN2", target_bir_lowering=False, num_devices=1)
    args = {k: nc.dram_tensor(f"in_{k}", a.shape, mybir.dt.from_np(a.dtype), kind="ExternalInput").ap()
            for k, a in arrays.items()}
    out = nc.dram_tensor("out_rows", (BATCH, BLOCKS, P, TILES, DIM), F32, kind="ExternalOutput").ap()
    build(nc, **args, out=out)
    r = run_bass_kernel_spmd(nc, [{f"in_{k}": a for k, a in arrays.items()}], core_ids=[0])
    got = np.asarray(r.results[0]["out_rows"])
    return np.ascontiguousarray(got.transpose(0, 1, 3, 2, 4)).reshape(BATCH, SEQ, DIM)
```

```python
import math
from contextlib import ExitStack

import numpy as np

import concourse.bass as bass
from concourse import mybir

F32 = mybir.dt.float32
F16 = mybir.dt.float16
U8 = mybir.dt.uint8
ALU = mybir.AluOpType
ACT = mybir.ActivationFunctionType
AX = mybir.AxisListType

P = 128
BATCH, SEQ, DIM, KEYS = 2, 2048, 512, 77
HID = DIM
CH = DIM // P
TILES = 4
ROWS = TILES * P
GROUPS = BATCH * SEQ // ROWS
BLOCKS = GROUPS // BATCH
HALF = CH * DIM // 2
KK = BATCH * KEYS
LN_EPS = 1e-5
MASKED = 1e9
SM_SCALE = 1.0 / math.sqrt(HID)
H_SCALE = 256.0
W_SCALE = 4096.0
UNSCALE = 1.0 / (H_SCALE * W_SCALE)
ROUND = 1.5 * 2.0 ** 23
TURN_HI = 6.28125
TURN_LO = 2.0 * math.pi - TURN_HI
SIN_MAX = 3.1415925


def build(nc, x, xT, ctxT, mask, Wk, WqT, Wv, Wo, bq, bk, bv, bo, theta, theta_noise, phi, phi_noise, out):
    with ExitStack() as ctx:
        def sb(name, shape, dt=F32):
            return ctx.enter_context(nc.sbuf_tensor(name, shape, dt))

        def bank(name):
            return ctx.enter_context(nc.psum_tensor(name, [P, DIM], F32))

        def sem(name):
            return ctx.enter_context(nc.semaphore(name))

        wk = sb("wk", [P, CH, HID])
        wqT = sb("wqT", [P, CH, DIM])
        wv = sb("wv", [P, CH, HID])
        wo = sb("wo", [P, CH, DIM])
        ctx_t = sb("ctx_t", [P, CH, KK])
        mask8 = sb("mask8", [P, KK], U8)
        bias_q = sb("bias_q", [P, CH])
        bias_k = sb("bias_k", [P, CH])
        bias_v = sb("bias_v", [P, CH])
        bo_rows = sb("bo_rows", [KEYS, DIM])
        angle_w = [sb(f"angle_w{i}", [P, CH * DIM]) for i in range(2)]
        angle_n = [sb(f"angle_n{i}", [P, CH * DIM]) for i in range(2)]
        turns = sb("turns", [P, CH * DIM])

        ones_mean = sb("ones_mean", [P, P])
        bq_cols = sb("bq_cols", [P, CH, P])
        kT = sb("kT", [P, CH, KK])
        vT = sb("vT", [P, CH, KK])
        a_raw = sb("a_raw", [P, CH, KK])
        a_mid = sb("a_mid", [P, CH, KK])
        a_keys = sb("a_keys", [P, CH, KK])
        keep = sb("keep", [P, KK])
        keep_off = sb("keep_off", [P, KK])
        c_mid = sb("c_mid", [P, KK])
        c_keys = sb("c_keys", [P, KK])
        vw = sb("vw", [KEYS, BATCH, DIM])
        w_hi = [sb(f"w_hi{i}", [P, CH, DIM], F16) for i in range(2)]
        w_lo = [sb(f"w_lo{i}", [P, CH, DIM], F16) for i in range(2)]
        ident = sb("ident", [P, P])
        minus_half = sb("minus_half", [P, TILES])
        eps = sb("eps", [P, TILES])

        xb = [sb(f"xb{i}", [P, TILES, DIM]) for i in range(2)]
        xTb = sb("xTb", [P, CH, ROWS])
        stats1 = sb("stats1", [P, TILES, 6])
        mv1 = sb("mv1", [P, TILES, 2])
        veps1 = sb("veps1", [P, TILES])
        rstd1 = sb("rstd1", [P, TILES])
        logits = sb("logits", [P, TILES, KEYS])
        shifted = sb("shifted", [P, TILES, KEYS])
        top = sb("top", [P, TILES])
        probs = sb("probs", [P, TILES, KEYS])
        total = sb("total", [P, TILES])
        inv_total = sb("inv_total", [P, TILES])
        probsT = sb("probsT", [KEYS, ROWS])
        x2 = [sb(f"x2_{i}", [P, TILES, DIM]) for i in range(2)]
        stats2 = sb("stats2", [P, TILES, 6])
        mv2 = sb("mv2", [P, TILES, 2])
        veps2 = sb("veps2", [P, TILES])
        rstd2 = sb("rstd2", [P, TILES])
        h = [sb(f"h{i}", [P, DIM]) for i in range(2)]
        h_split = [sb(f"h_split{j}", [P, 2, DIM], F16) for j in range(TILES)]
        hT = [sb(f"hT{j}", [P, 2, CH, P], F16) for j in range(TILES)]
        sq_re = [sb(f"sq_re{i}", [P, DIM]) for i in range(2)]
        sq_im = [sb(f"sq_im{i}", [P, DIM]) for i in range(2)]
        power = sb("power", [P, TILES, DIM])
        result = sb("result", [P, TILES, DIM])

        re_bank = [bank("re0"), bank("re1")]
        im_bank = [bank("im0"), bank("im1")]
        score_bank = bank("score_bank")
        pT_bank = bank("pT_bank")
        att_bank = [bank("att0"), bank("att1")]
        prep = [re_bank[0], re_bank[1], im_bank[0], im_bank[1], score_bank, pT_bank, att_bank[0], att_bank[1]]

        ld_ctx, ld_wk, ld_wq, ld_wv, ld_wo = (sem(f"ld_{n}") for n in ("ctx", "wk", "wq", "wv", "wo"))
        ld_bq, ld_bk, ld_bv, ld_bo, ld_mask = (sem(f"ld_{n}") for n in ("bq", "bk", "bv", "bo", "mask"))
        ld_angle = [[sem(f"ld_{n}{half}") for half in range(2)] for n in ("theta", "phi")]
        consts_made = sem("consts_made")
        v_consts = sem("v_consts")
        kT_mm, kT_ready = sem("kT_mm"), sem("kT_ready")
        a_mm, a_copied = sem("a_mm"), sem("a_copied")
        c_mm, mean_mm = sem("c_mm"), sem("mean_mm")
        a_centred, keys_ready = sem("a_centred"), sem("keys_ready")
        vT_mm, vT_ready = sem("vT_mm"), sem("vT_ready")
        vw_mm, vw_ready = sem("vw_mm"), sem("vw_ready")
        angle_summed = [sem("theta_summed"), sem("phi_summed")]
        turns_rounded, turns_made = sem("turns_rounded"), sem("turns_made")
        angle_step = sem("angle_step")
        angle_ready = sem("angle_ready")
        sine_made = sem("sine_made")
        w_hi_ready, w_ready = sem("w_hi_ready"), sem("w_ready")
        x_loaded = [sem("x_loaded0"), sem("x_loaded1")]
        xT_loaded, stored = sem("xT_loaded"), sem("stored")
        stats1_made, mean1_made, eps1_added, rstd1_made = (sem(f"{n}") for n in ("stats1_made", "mean1_made", "eps1_added", "rstd1_made"))
        scores_mm, scores_read, top_found, shifted_made = (sem(f"{n}") for n in ("scores_mm", "scores_read", "top_found", "shifted_made"))
        probs_made, total_made, inv_total_made = sem("probs_made"), sem("total_made"), sem("inv_total_made")
        pT_mm, pT_copied = sem("pT_mm"), sem("pT_copied")
        att_mm, x2_made = sem("att_mm"), sem("x2_made")
        stats2_made, mean2_made, eps2_added, rstd2_made = (sem(f"{n}") for n in ("stats2_made", "mean2_made", "eps2_added", "rstd2_made"))
        h_made, hi_made, lo_made = sem("h_made"), sem("hi_made"), sem("lo_made")
        transposes_sent = sem("transposes_sent")
        hT_ready = [sem(f"hT_ready{j}") for j in range(TILES)]
        re_mm, im_mm, re_squared, im_squared, power_made = (sem(f"{n}") for n in ("re_mm", "im_mm", "re_squared", "im_squared", "power_made"))
        root_made, result_made = sem("root_made"), sem("result_made")

        LAST = GROUPS - 1

        block = ctx.enter_context(nc.Block())

        @block.sync
        def _(sp):
            def load_x(batch, blk):
                sp.dma_start(xb[batch][:, :, :], x[batch, blk]).then_inc(x_loaded[batch], 16)

            def load_xT(batch, blk):
                sp.dma_start(xTb[:, :, :], xT[batch, blk]).then_inc(xT_loaded, 16)

            def load_angles(part, half):
                cols_ = slice(HALF * half, HALF * half + HALF)
                w_dram, n_dram = ((theta, theta_noise), (phi, phi_noise))[part]
                sp.dma_start(angle_w[part][:, cols_], w_dram[:, cols_]).then_inc(ld_angle[part][half], 16)
                sp.dma_start(angle_n[part][:, cols_], n_dram[:, cols_]).then_inc(ld_angle[part][half], 16)

            sp.dma_start(ctx_t[:, :, :], ctxT).then_inc(ld_ctx, 16)
            sp.dma_start(wk[:, :, :], Wk).then_inc(ld_wk, 16)
            load_angles(0, 0)
            load_angles(0, 1)
            sp.dma_start(wqT[:, :, :], WqT).then_inc(ld_wq, 16)
            sp.dma_start(wv[:, :, :], Wv).then_inc(ld_wv, 16)
            load_angles(1, 0)
            load_xT(0, 0)
            load_x(0, 0)
            sp.dma_start(wo[:, :, :], Wo).then_inc(ld_wo, 16)
            load_angles(1, 1)
            load_x(1, 0)
            sp.wait_ge(scores_mm, 1)
            load_xT(1, 0)

            def transpose_h(m, tiles):
                for j in tiles:
                    sp.wait_ge(lo_made, TILES * m + j + 1)
                    sp.sem_inc(transposes_sent, 1)
                    sp.dma_start_transpose(hT[j][:, :, :, :].rearrange("p s c r -> p (s c) r"),
                                           h_split[j][:, :, :].rearrange("p s d -> p (s d)")).then_inc(hT_ready[j], 16)

            def step(n, batch, blk, load, store):
                if not isinstance(n, int) or n > 0:
                    transpose_h(n, [TILES - 1])
                if load:
                    sp.wait_ge(x2_made, TILES * (n + 1))
                    load_x(batch, blk)
                    sp.wait_ge(scores_mm, n + 2)
                    load_xT(batch, blk)
                if store:
                    sp.wait_ge(result_made, n)
                    sp.dma_start(out[1 - batch, blk - 1 - (1 - batch)], result[:, :, :]).then_inc(stored, 16)
                if not isinstance(n, int) or n < LAST:
                    transpose_h(n + 1, range(TILES - 1))

            transpose_h(0, range(TILES))
            step(0, 0, 1, True, False)
            with sp.Fori(0, 2) as i:
                step(2 * i + 1, 1, i + 1, True, True)
                step(2 * i + 2, 0, i + 2, True, True)
            step(5, 1, 3, True, True)
            step(6, 0, 4, False, True)
            step(7, 1, 4, False, True)
            for j in range(TILES):
                sp.wait_ge(result_made, LAST + j + 1)
                sp.dma_start(out[1, BLOCKS - 1, :, j, :], result[:, j, :]).then_inc(stored, 16)
            sp.wait_ge(stored, 16 * (LAST + TILES))

        @block.gpsimd
        def _(pool):
            nc.gpsimd.memset(minus_half[:, :], -0.5)
            nc.gpsimd.memset(eps[:, :], LN_EPS)
            nc.gpsimd.memset(ident[:, :], 0.0).then_inc(consts_made, 1)
            pool.wait_ge(consts_made, 1)
            nc.gpsimd.affine_select(out=ident[:, :], in_=ident[:, :], compare_op=ALU.not_equal, fill=1.0,
                                    base=0, pattern=[[-1, P]], channel_multiplier=1).then_inc(consts_made, 1)

            def sum_angle(half):
                pool.wait_ge(ld_angle[1][half], 32)
                cols_ = slice(HALF * half, HALF * half + HALF)
                nc.gpsimd.tensor_tensor(angle_w[1][:, cols_], angle_w[1][:, cols_], angle_n[1][:, cols_],
                                        ALU.add).then_inc(angle_summed[1], 1)

            def rstd_of_x(m):
                pool.wait_ge(mean1_made, m + 1)
                nc.gpsimd.tensor_tensor(veps1[:, :], mv1[:, :, 1], eps[:, :], ALU.add).then_inc(eps1_added, 1)
                pool.wait_ge(eps1_added, m + 1)
                nc.gpsimd.tensor_tensor(rstd1[:, :], veps1[:, :], minus_half[:, :], ALU.pow).then_inc(rstd1_made, 1)

            def rstd_of_x2(m, j):
                pool.wait_ge(mean2_made, TILES * m + j + 1)
                nc.gpsimd.tensor_tensor(veps2[:, j:j + 1], mv2[:, j, 1:2], eps[:, 0:1], ALU.add).then_inc(eps2_added, 1)
                pool.wait_ge(eps2_added, TILES * m + j + 1)
                nc.gpsimd.tensor_tensor(rstd2[:, j:j + 1], veps2[:, j:j + 1], minus_half[:, 0:1], ALU.pow).then_inc(rstd2_made, 1)

            def step(m):
                rstd_of_x(m + 1)
                for j in range(TILES):
                    rstd_of_x2(m, j)

            sum_angle(0)
            rstd_of_x(0)
            sum_angle(1)
            for j in range(TILES):
                rstd_of_x2(0, j)
            rstd_of_x(1)
            with pool.Fori(0, 3) as i:
                step(2 * i + 1)
                step(2 * i + 2)
            for j in range(TILES):
                rstd_of_x2(LAST, j)

        @block.tensor
        def _(pe):
            pe.wait_ge(ld_ctx, 16)
            pe.wait_ge(ld_wk, 16)
            for c in range(CH):
                for k in range(CH):
                    last = nc.tensor.matmul(prep[c][:, 0:KK], wk[:, k, P * c:P * c + P], ctx_t[:, k, :],
                                            start=(k == 0), stop=(k == CH - 1))
                last.then_inc(kT_mm, 1)
            pe.wait_ge(ld_wq, 16)
            pe.wait_ge(kT_ready, CH)
            for c in range(CH):
                for k in range(CH):
                    last = nc.tensor.matmul(prep[4 + c][:, 0:KK], wqT[:, k, P * c:P * c + P], kT[:, k, :],
                                            start=(k == 0), stop=(k == CH - 1))
                last.then_inc(a_mm, 1)
            pe.wait_ge(v_consts, 3)
            for k in range(CH):
                last = nc.tensor.matmul(prep[0][:, 0:KK], bq_cols[:, k, :], kT[:, k, :],
                                        start=(k == 0), stop=(k == CH - 1))
            last.then_inc(c_mm, 1)
            pe.wait_ge(a_copied, CH)
            for k in range(CH):
                last = nc.tensor.matmul(prep[1][:, 0:KK], ones_mean[:, :], a_raw[:, k, :],
                                        start=(k == 0), stop=(k == CH - 1))
            last.then_inc(mean_mm, 1)

            def scores(m, batch):
                pe.wait_ge(xT_loaded, 16 * (m + 1))
                if not isinstance(m, int) or m > 0:
                    pe.wait_ge(scores_read, m)
                for j in range(TILES):
                    for k in range(CH):
                        last = nc.tensor.matmul(score_bank[:, KEYS * j:KEYS * j + KEYS], xTb[:, k, P * j:P * j + P],
                                                a_keys[:, k, KEYS * batch:KEYS * batch + KEYS],
                                                start=(k == 0), stop=(k == CH - 1))
                last.then_inc(scores_mm, 1)

            def transpose_probs(m):
                pe.wait_ge(probs_made, m + 1)
                if not isinstance(m, int) or m > 0:
                    pe.wait_ge(pT_copied, m)
                for j in range(TILES):
                    last = nc.tensor.transpose(pT_bank[0:KEYS, P * j:P * j + P], probs[:, j, :], ident[:, :])
                last.then_inc(pT_mm, 1)

            def attend(m, batch, j):
                pe.wait_ge(pT_copied, m + 1)
                if j >= 2 or not isinstance(m, int) or m > 0:
                    pe.wait_ge(x2_made, TILES * m + j - 1)
                nc.tensor.matmul(att_bank[j % 2][:, :], probsT[:, P * j:P * j + P], vw[:, batch, :],
                                 start=True, stop=True).then_inc(att_mm, 1)

            def feed(n, j, part):
                bank_ = (re_bank, im_bank)[part][j % 2]
                pe.wait_ge(hT_ready[j], 16 * (n + 1))
                if j >= 2 or not isinstance(n, int) or n > 0:
                    pe.wait_ge((re_squared, im_squared)[part], TILES * n + j - 1)
                for k in range(CH):
                    nc.tensor.matmul(bank_[:, :], hT[j][:, 0, k, :], w_hi[part][:, k, :], start=(k == 0), stop=False)
                    nc.tensor.matmul(bank_[:, :], hT[j][:, 0, k, :], w_lo[part][:, k, :], start=False, stop=False)
                    last = nc.tensor.matmul(bank_[:, :], hT[j][:, 1, k, :], w_hi[part][:, k, :],
                                            start=False, stop=(k == CH - 1))
                last.then_inc((re_mm, im_mm)[part], 1)

            def project_values(b):
                for k in range(CH):
                    last = nc.tensor.matmul(prep[b][0:KEYS, :], vT[:, k, KEYS * b:KEYS * b + KEYS], wo[:, k, :],
                                            start=(k == 0), stop=(k == CH - 1))
                last.then_inc(vw_mm, 1)

            pe.wait_ge(ld_wv, 16)
            for c in range(CH):
                bank_ = prep[2 + c] if c < 2 else prep[3 + c]
                for k in range(CH):
                    last = nc.tensor.matmul(bank_[:, 0:KK], wv[:, k, P * c:P * c + P], ctx_t[:, k, :],
                                            start=(k == 0), stop=(k == CH - 1))
                last.then_inc(vT_mm, 1)
            pe.wait_ge(keys_ready, 2)
            scores(0, 0)
            pe.wait_ge(ld_wo, 16)
            pe.wait_ge(vT_ready, CH)
            project_values(0)
            pe.wait_ge(consts_made, 2)
            transpose_probs(0)
            pe.wait_ge(vw_ready, 1)
            attend(0, 0, 0)
            attend(0, 0, 1)
            project_values(1)
            attend(0, 0, 2)
            attend(0, 0, 3)
            scores(1, 1)

            def step(n, batch):
                scores(n + 1, batch)
                feed(n, 0, 0)
                feed(n, 0, 1)
                feed(n, 1, 0)
                transpose_probs(n + 1)
                feed(n, 1, 1)
                attend(n + 1, batch, 0)
                feed(n, 2, 0)
                attend(n + 1, batch, 1)
                feed(n, 2, 1)
                attend(n + 1, batch, 2)
                feed(n, 3, 0)
                attend(n + 1, batch, 3)
                feed(n, 3, 1)

            pe.wait_ge(w_ready, 2)
            feed(0, 0, 0)
            pe.wait_ge(vw_ready, 2)
            feed(0, 1, 0)
            pe.wait_ge(w_ready, 4)
            feed(0, 0, 1)
            feed(0, 1, 1)
            feed(0, 2, 0)
            transpose_probs(1)
            feed(0, 2, 1)
            attend(1, 1, 0)
            attend(1, 1, 1)
            feed(0, 3, 0)
            attend(1, 1, 2)
            feed(0, 3, 1)
            attend(1, 1, 3)
            with pe.Fori(0, 3) as i:
                step(2 * i + 1, 0)
                step(2 * i + 2, 1)
            for j in range(TILES):
                feed(LAST, j, 0)
                feed(LAST, j, 1)

        @block.scalar
        def _(act):
            act.dma_start(bias_k[:, :], bk).then_inc(ld_bk, 16)
            act.dma_start(bias_q[:, :], bq).then_inc(ld_bq, 16)
            act.dma_start(mask8[:, :], mask).then_inc(ld_mask, 16)
            act.dma_start(bias_v[:, :], bv).then_inc(ld_bv, 16)
            act.dma_start(bo_rows[:, :], bo).then_inc(ld_bo, 16)
            act.wait_ge(ld_bk, 16)
            for c in range(CH):
                act.wait_ge(kT_mm, c + 1)
                nc.scalar.activation(kT[:, c, :], prep[c][:, 0:KK], ACT.Identity,
                                     bias=bias_k[:, c:c + 1]).then_inc(kT_ready, 1)
            def turns_of(part, half):
                u = 2 * part + half
                act.wait_ge(angle_summed[part], half + 1)
                if part:
                    act.wait_ge(angle_step, 2 * half + 2)
                cols_ = slice(HALF * half, HALF * half + HALF)
                nc.scalar.activation(turns[:, cols_], angle_w[part][:, cols_], ACT.Copy,
                                     bias=ROUND, scale=1.0 / (2.0 * math.pi)).then_inc(turns_rounded, 1)
                act.wait_ge(turns_rounded, u + 1)
                nc.scalar.activation(turns[:, cols_], turns[:, cols_], ACT.Copy, bias=-ROUND).then_inc(turns_made, 1)

            def sine(part, half):
                u = 2 * part + half
                act.wait_ge(angle_ready, u + 1)
                cols_ = slice(HALF * half, HALF * half + HALF)
                nc.scalar.activation(angle_n[part][:, cols_], angle_w[part][:, cols_], ACT.Sin).then_inc(sine_made, 1)
                act.wait_ge(sine_made, u + 1)
                nc.scalar.activation(w_hi[part][:, :, :].rearrange("p c d -> p (c d)")[:, cols_], angle_n[part][:, cols_],
                                     ACT.Copy, scale=W_SCALE).then_inc(w_hi_ready, 1)

            def exps(m):
                act.wait_ge(shifted_made, m + 1)
                if not isinstance(m, int) or m > 0:
                    act.wait_ge(pT_mm, m)
                    act.wait_ge(total_made, m)
                nc.scalar.activation(probs[:, :, :], shifted[:, :, :], ACT.Exp).then_inc(probs_made, 1)

            def copy_pT(m):
                act.wait_ge(pT_mm, m + 1)
                if not isinstance(m, int) or m > 0:
                    act.wait_ge(att_mm, TILES * m)
                nc.scalar.activation(probsT[:, :], pT_bank[0:KEYS, :], ACT.Copy).then_inc(pT_copied, 1)

            def high_half(m, j):
                act.wait_ge(h_made, TILES * m + j + 1)
                if not isinstance(m, int) or m > 0:
                    act.wait_ge(hT_ready[j], 16 * m)
                nc.scalar.activation(h_split[j][:, 0, :], h[j % 2][:, :], ACT.Copy, scale=H_SCALE).then_inc(hi_made, 1)

            def square(n, j, part):
                act.wait_ge((re_mm, im_mm)[part], TILES * n + j + 1)
                if j >= 2 or not isinstance(n, int) or n > 0:
                    act.wait_ge(power_made, TILES * n + j - 1)
                nc.scalar.activation((sq_re, sq_im)[part][j % 2][:, :], (re_bank, im_bank)[part][j % 2][:, :],
                                     ACT.Square, scale=UNSCALE).then_inc((re_squared, im_squared)[part], 1)

            def roots(n):
                act.wait_ge(power_made, TILES * (n + 1))
                nc.scalar.activation(power[:, :, :], power[:, :, :], ACT.Sqrt).then_inc(root_made, 1)

            turns_of(0, 0)
            turns_of(0, 1)
            for c in range(CH):
                act.wait_ge(a_mm, c + 1)
                nc.scalar.activation(a_raw[:, c, :], prep[4 + c][:, 0:KK], ACT.Copy, scale=SM_SCALE).then_inc(a_copied, 1)
                if c == 0:
                    sine(0, 0)
            sine(0, 1)
            act.wait_ge(ld_bv, 16)
            for c in range(CH):
                bank_ = prep[2 + c] if c < 2 else prep[3 + c]
                act.wait_ge(vT_mm, c + 1)
                nc.scalar.activation(vT[:, c, :], bank_[:, 0:KK], ACT.Identity,
                                     bias=bias_v[:, c:c + 1]).then_inc(vT_ready, 1)
            turns_of(1, 0)
            exps(0)
            copy_pT(0)
            turns_of(1, 1)
            sine(1, 0)
            high_half(0, 0)
            sine(1, 1)
            high_half(0, 1)
            high_half(0, 2)
            high_half(0, 3)
            square(0, 0, 0)
            square(0, 1, 0)
            square(0, 0, 1)
            exps(1)
            square(0, 1, 1)
            square(0, 2, 0)
            copy_pT(1)
            square(0, 2, 1)
            high_half(1, 0)
            high_half(1, 1)
            square(0, 3, 0)
            high_half(1, 2)

            def step(n):
                square(n - 1, 3, 1)
                high_half(n, 3)
                roots(n - 1)
                exps(n + 1)
                square(n, 0, 0)
                square(n, 0, 1)
                square(n, 1, 0)
                copy_pT(n + 1)
                square(n, 1, 1)
                square(n, 2, 0)
                high_half(n + 1, 0)
                square(n, 2, 1)
                high_half(n + 1, 1)
                square(n, 3, 0)
                high_half(n + 1, 2)

            with act.Fori(0, 3) as i:
                step(2 * i + 1)
                step(2 * i + 2)
            square(LAST - 1, 3, 1)
            high_half(LAST, 3)
            roots(LAST - 1)
            for j in range(TILES):
                square(LAST, j, 0)
                square(LAST, j, 1)
                act.wait_ge(power_made, TILES * LAST + j + 1)
                nc.scalar.activation(power[:, j, :], power[:, j, :], ACT.Sqrt).then_inc(root_made, 1)

        @block.vector
        def _(dve):
            nc.vector.memset(ones_mean[:, :], 1.0 / DIM).then_inc(v_consts, 1)
            nc.vector.memset(bq_cols[:, :, :], SM_SCALE).then_inc(v_consts, 1)
            dve.wait_ge(ld_bq, 16)
            dve.wait_ge(v_consts, 2)
            nc.vector.tensor_tensor(bq_cols[:, :, :], bq_cols[:, :, :],
                                    bias_q[:, :].unsqueeze(2).to_broadcast([P, CH, P]), ALU.mult).then_inc(v_consts, 1)
            dve.wait_ge(ld_mask, 16)
            nc.vector.tensor_copy(keep[:, :], mask8[:, :]).then_inc(v_consts, 1)
            dve.wait_ge(v_consts, 4)
            nc.vector.tensor_scalar(keep_off[:, :], keep[:, :], MASKED, -MASKED, ALU.mult, ALU.add).then_inc(v_consts, 1)

            def sum_angle(half):
                dve.wait_ge(ld_angle[0][half], 32)
                cols_ = slice(HALF * half, HALF * half + HALF)
                nc.vector.scalar_tensor_tensor(out=angle_w[0][:, cols_], in0=angle_w[0][:, cols_], scalar=0.5 * math.pi,
                                               in1=angle_n[0][:, cols_], op0=ALU.add,
                                               op1=ALU.add).then_inc(angle_summed[0], 1)

            def reduce_angle(part, half):
                u = 2 * part + half
                w = angle_w[part][:, HALF * half:HALF * half + HALF]
                k = turns[:, HALF * half:HALF * half + HALF]
                dve.wait_ge(turns_made, u + 1)
                nc.vector.scalar_tensor_tensor(out=w, in0=k, scalar=-TURN_HI, in1=w,
                                               op0=ALU.mult, op1=ALU.add).then_inc(angle_step, 1)
                dve.wait_ge(angle_step, 2 * u + 1)
                nc.vector.scalar_tensor_tensor(out=w, in0=k, scalar=-TURN_LO, in1=w,
                                               op0=ALU.mult, op1=ALU.add).then_inc(angle_step, 1)
                dve.wait_ge(angle_step, 2 * u + 2)
                nc.vector.tensor_scalar(w, w, SIN_MAX, -SIN_MAX, ALU.min, ALU.max).then_inc(angle_ready, 1)

            def low_half_of_sine(part, half):
                dve.wait_ge(w_hi_ready, 2 * part + half + 1)
                cols_ = slice(HALF * half, HALF * half + HALF)
                nc.vector.scalar_tensor_tensor(
                    out=w_lo[part][:, :, :].rearrange("p c d -> p (c d)")[:, cols_], in0=angle_n[part][:, cols_],
                    scalar=W_SCALE, in1=w_hi[part][:, :, :].rearrange("p c d -> p (c d)")[:, cols_],
                    op0=ALU.mult, op1=ALU.subtract).then_inc(w_ready, 1)

            def stats_of_x(b, blk):
                dve.wait_ge(x_loaded[b], 16 * (blk + 1))
                for j in range(TILES):
                    last = nc.vector.bn_stats(stats1[:, j, :], xb[b][:, j, :])
                last.then_inc(stats1_made, 1)

            def mean_of_x(m):
                for j in range(TILES):
                    last = nc.vector.bn_aggr(mv1[:, j, :], stats1[:, j, :])
                last.then_inc(mean1_made, 1)

            def softmax_shift(m, b):
                dve.wait_ge(scores_mm, m + 1)
                dve.wait_ge(rstd1_made, m + 1)
                if not isinstance(m, int) or m > 0:
                    dve.wait_ge(shifted_made, m)
                for j in range(TILES):
                    last = nc.vector.scalar_tensor_tensor(
                        out=logits[:, j, :], in0=score_bank[:, KEYS * j:KEYS * j + KEYS], scalar=rstd1[:, j:j + 1],
                        in1=c_keys[:, KEYS * b:KEYS * b + KEYS], op0=ALU.mult, op1=ALU.add)
                last.then_inc(scores_read, 1)
                dve.wait_ge(scores_read, m + 1)
                nc.vector.tensor_reduce(top[:, :], logits[:, :, :], AX.X, ALU.max).then_inc(top_found, 1)
                dve.wait_ge(top_found, m + 1)
                if not isinstance(m, int) or m > 0:
                    dve.wait_ge(probs_made, m)
                nc.vector.tensor_tensor(shifted[:, :, :], logits[:, :, :],
                                        top[:, :].unsqueeze(2).to_broadcast([P, TILES, KEYS]),
                                        ALU.subtract).then_inc(shifted_made, 1)

            def softmax_total(m):
                dve.wait_ge(probs_made, m + 1)
                if not isinstance(m, int) or m > 0:
                    dve.wait_ge(inv_total_made, m)
                nc.vector.tensor_reduce(total[:, :], probs[:, :, :], AX.X, ALU.add).then_inc(total_made, 1)
                dve.wait_ge(total_made, m + 1)
                if not isinstance(m, int) or m > 0:
                    dve.wait_ge(x2_made, TILES * m)
                nc.vector.reciprocal(inv_total[:, :], total[:, :]).then_inc(inv_total_made, 1)

            def residual(m, b, j):
                dve.wait_ge(att_mm, TILES * m + j + 1)
                dve.wait_ge(inv_total_made, m + 1)
                if not isinstance(m, int) or m > 1:
                    dve.wait_ge(result_made, m - 1)
                nc.vector.scalar_tensor_tensor(out=x2[b][:, j, :], in0=att_bank[j % 2][:, :], scalar=inv_total[:, j:j + 1],
                                               in1=xb[b][:, j, :], op0=ALU.mult, op1=ALU.add).then_inc(x2_made, 1)
                dve.wait_ge(x2_made, TILES * m + j + 1)
                nc.vector.bn_stats(stats2[:, j, :], x2[b][:, j, :]).then_inc(stats2_made, 1)

            def stats_ready(m, j):
                dve.wait_ge(stats2_made, TILES * m + j + 1)

            def mean_of_x2(m, j):
                nc.vector.bn_aggr(mv2[:, j, :], stats2[:, j, :]).then_inc(mean2_made, 1)

            def normalise(m, b, j):
                dve.wait_ge(rstd2_made, TILES * m + j + 1)
                if j >= 2 or not isinstance(m, int) or m > 0:
                    dve.wait_ge(lo_made, TILES * m + j - 1)
                nc.vector.tensor_scalar(h[j % 2][:, :], x2[b][:, j, :], mv2[:, j, 0:1], rstd2[:, j:j + 1],
                                        ALU.subtract, ALU.mult).then_inc(h_made, 1)

            def low_half(m, j):
                dve.wait_ge(hi_made, TILES * m + j + 1)
                nc.vector.scalar_tensor_tensor(out=h_split[j][:, 1, :], in0=h[j % 2][:, :],
                                               scalar=H_SCALE, in1=h_split[j][:, 0, :],
                                               op0=ALU.mult, op1=ALU.subtract).then_inc(lo_made, 1)

            def add_squares(n, j):
                dve.wait_ge(re_squared, TILES * n + j + 1)
                dve.wait_ge(im_squared, TILES * n + j + 1)
                if not isinstance(n, int) or n > 0:
                    dve.wait_ge(result_made, n)
                nc.vector.tensor_tensor(power[:, j, :], sq_re[j % 2][:, :], sq_im[j % 2][:, :],
                                        ALU.add).then_inc(power_made, 1)

            def finish(n, b):
                dve.wait_ge(root_made, n + 1)
                if not isinstance(n, int) or n > 0:
                    dve.wait_ge(stored, 16 * n)
                nc.vector.tensor_tensor(result[:, :, :], x2[b][:, :, :], power[:, :, :], ALU.add).then_inc(result_made, 1)

            sum_angle(0)
            sum_angle(1)
            reduce_angle(0, 0)
            reduce_angle(0, 1)
            low_half_of_sine(0, 0)
            dve.wait_ge(mean_mm, 1)
            nc.vector.tensor_tensor(a_mid[:, :, :], a_raw[:, :, :],
                                    prep[1][:, 0:KK].unsqueeze(1).to_broadcast([P, CH, KK]),
                                    ALU.subtract).then_inc(a_centred, 1)
            dve.wait_ge(c_mm, 1)
            nc.vector.tensor_tensor(c_mid[:, :], prep[0][:, 0:KK], keep[:, :], ALU.mult).then_inc(a_centred, 1)
            dve.wait_ge(a_centred, 2)
            nc.vector.tensor_tensor(a_keys[:, :, :], a_mid[:, :, :],
                                    keep[:, :].unsqueeze(1).to_broadcast([P, CH, KK]), ALU.mult).then_inc(keys_ready, 1)
            dve.wait_ge(v_consts, 5)
            nc.vector.tensor_tensor(c_keys[:, :], c_mid[:, :], keep_off[:, :], ALU.add).then_inc(keys_ready, 1)
            low_half_of_sine(0, 1)
            stats_of_x(0, 0)
            dve.wait_ge(stats1_made, 1)
            mean_of_x(0)

            def values_ready(b):
                dve.wait_ge(vw_mm, b + 1)
                nc.vector.tensor_tensor(vw[:, b, :], prep[b][0:KEYS, :], bo_rows[:, :], ALU.add).then_inc(vw_ready, 1)

            reduce_angle(1, 0)
            softmax_shift(0, 0)
            softmax_total(0)
            dve.wait_ge(ld_bo, 16)
            values_ready(0)
            residual(0, 0, 0)
            stats_ready(0, 0)
            mean_of_x2(0, 0)
            reduce_angle(1, 1)
            residual(0, 0, 1)
            stats_ready(0, 1)
            normalise(0, 0, 0)
            mean_of_x2(0, 1)
            values_ready(1)
            low_half(0, 0)
            residual(0, 0, 2)
            stats_ready(0, 2)
            normalise(0, 0, 1)
            mean_of_x2(0, 2)
            residual(0, 0, 3)
            stats_ready(0, 3)
            low_half(0, 1)
            mean_of_x2(0, 3)
            normalise(0, 0, 2)
            low_half_of_sine(1, 0)
            low_half(0, 2)
            normalise(0, 0, 3)
            low_half_of_sine(1, 1)
            low_half(0, 3)
            stats_of_x(1, 0)
            dve.wait_ge(stats1_made, 2)
            add_squares(0, 0)
            mean_of_x(1)
            softmax_shift(1, 1)
            add_squares(0, 1)
            softmax_total(1)
            stats_of_x(0, 1)
            residual(1, 1, 0)
            stats_ready(1, 0)
            dve.wait_ge(stats1_made, 3)
            add_squares(0, 2)
            mean_of_x(2)
            mean_of_x2(1, 0)
            residual(1, 1, 1)
            stats_ready(1, 1)
            normalise(1, 1, 0)
            mean_of_x2(1, 1)
            low_half(1, 0)
            residual(1, 1, 2)
            stats_ready(1, 2)
            normalise(1, 1, 1)
            mean_of_x2(1, 2)
            low_half(1, 1)
            residual(1, 1, 3)
            stats_ready(1, 3)
            normalise(1, 1, 2)
            mean_of_x2(1, 3)
            low_half(1, 2)
            normalise(1, 1, 3)

            def step(n, b, blk):
                m, a = n + 1, 1 - b
                add_squares(n - 1, 3)
                low_half(n, 3)
                softmax_shift(m, a)
                finish(n - 1, a)
                softmax_total(m)
                add_squares(n, 0)
                if blk is not None:
                    stats_of_x(b, blk)
                    dve.wait_ge(stats1_made, m + 2)
                add_squares(n, 1)
                if blk is not None:
                    mean_of_x(m + 1)
                residual(m, a, 0)
                stats_ready(m, 0)
                residual(m, a, 1)
                mean_of_x2(m, 0)
                stats_ready(m, 1)
                normalise(m, a, 0)
                mean_of_x2(m, 1)
                add_squares(n, 2)
                low_half(m, 0)
                residual(m, a, 2)
                stats_ready(m, 2)
                normalise(m, a, 1)
                mean_of_x2(m, 2)
                low_half(m, 1)
                residual(m, a, 3)
                stats_ready(m, 3)
                normalise(m, a, 2)
                mean_of_x2(m, 3)
                low_half(m, 2)
                normalise(m, a, 3)

            with dve.Fori(0, 2) as i:
                step(2 * i + 1, 1, i + 1)
                step(2 * i + 2, 0, i + 2)
            step(5, 1, 3)
            step(6, 0, None)
            add_squares(LAST - 1, 3)
            low_half(LAST, 3)
            finish(LAST - 1, 0)
            for j in range(TILES):
                add_squares(LAST, j)
                dve.wait_ge(root_made, LAST + j + 1)
                dve.wait_ge(stored, 16 * LAST)
                nc.vector.tensor_tensor(result[:, j, :], x2[1][:, j, :], power[:, j, :], ALU.add).then_inc(result_made, 1)


def kernel(x, ctx_1024, mask_BxS2_bk0, L0_xattn_Wq, L0_xattn_bq, L0_xattn_Wk, L0_xattn_bk, L0_xattn_Wv, L0_xattn_bv,
           L0_xattn_Wo, L0_xattn_bo, L0_ffn_theta, L0_ffn_phi, L0_ffn_theta_noise, L0_ffn_phi_noise):
    import concourse.bacc as bacc
    from concourse.bass_utils import run_bass_kernel_spmd

    def cols(w):
        w = np.asarray(w)
        return np.ascontiguousarray(w.reshape(CH, P, -1).transpose(1, 0, 2))

    rows = np.asarray(x).reshape(BATCH, BLOCKS, TILES, P, DIM)
    arrays = {
        "x": np.ascontiguousarray(rows.transpose(0, 1, 3, 2, 4)),
        "xT": np.ascontiguousarray(np.asarray(x).reshape(BATCH, BLOCKS, ROWS, CH, P).transpose(0, 1, 4, 3, 2)),
        "ctxT": cols(np.asarray(ctx_1024).reshape(KK, DIM).T),
        "mask": np.ascontiguousarray(np.broadcast_to(np.asarray(mask_BxS2_bk0).reshape(1, KK), (P, KK))),
        "Wk": cols(L0_xattn_Wk),
        "WqT": cols(np.asarray(L0_xattn_Wq).T),
        "Wv": cols(L0_xattn_Wv),
        "Wo": cols(L0_xattn_Wo),
        "bq": np.ascontiguousarray(np.asarray(L0_xattn_bq).reshape(CH, P).T),
        "bk": np.ascontiguousarray(np.asarray(L0_xattn_bk).reshape(CH, P).T),
        "bv": np.ascontiguousarray(np.asarray(L0_xattn_bv).reshape(CH, P).T),
        "bo": np.ascontiguousarray(np.broadcast_to(np.asarray(L0_xattn_bo).reshape(1, DIM), (KEYS, DIM))),
        "theta": cols(L0_ffn_theta).reshape(P, CH * DIM),
        "theta_noise": cols(L0_ffn_theta_noise).reshape(P, CH * DIM),
        "phi": cols(L0_ffn_phi).reshape(P, CH * DIM),
        "phi_noise": cols(L0_ffn_phi_noise).reshape(P, CH * DIM),
    }
    nc = bacc.Bacc("TRN2", target_bir_lowering=False, num_devices=1)
    args = {k: nc.dram_tensor(f"in_{k}", a.shape, mybir.dt.from_np(a.dtype), kind="ExternalInput").ap()
            for k, a in arrays.items()}
    out = nc.dram_tensor("out_rows", (BATCH, BLOCKS, P, TILES, DIM), F32, kind="ExternalOutput").ap()
    build(nc, **args, out=out)
    r = run_bass_kernel_spmd(nc, [{f"in_{k}": a for k, a in arrays.items()}], core_ids=[0])
    got = np.asarray(r.results[0]["out_rows"])
    return np.ascontiguousarray(got.transpose(0, 1, 3, 2, 4)).reshape(BATCH, SEQ, DIM)
```

```python
import math
from contextlib import ExitStack

import numpy as np

import concourse.bass as bass
from concourse import mybir

F32 = mybir.dt.float32
F16 = mybir.dt.float16
U8 = mybir.dt.uint8
ALU = mybir.AluOpType
ACT = mybir.ActivationFunctionType
AX = mybir.AxisListType

P = 128
BATCH, SEQ, DIM, KEYS = 2, 2048, 512, 77
HID = DIM
CH = DIM // P
TILES = 4
ROWS = TILES * P
GROUPS = BATCH * SEQ // ROWS
BLOCKS = GROUPS // BATCH
HALF = CH * DIM // 2
KK = BATCH * KEYS
LN_EPS = 1e-5
MASKED = 1e9
SM_SCALE = 1.0 / math.sqrt(HID)
H_SCALE = 256.0
W_SCALE = 4096.0
UNSCALE = 1.0 / (H_SCALE * W_SCALE)
P_SCALE = 4096.0
V_SCALE = 8192.0
TINY = 1e-30
STACK = 3 * KEYS
REST = STACK - P
ROUND = 1.5 * 2.0 ** 23
TURN_HI = 6.28125
TURN_LO = 2.0 * math.pi - TURN_HI
SIN_MAX = 3.1415925


def build(nc, x, xT, ctxT, mask, Wk, WqT, Wv, Wo, bq, bk, bv, bo, theta, theta_noise, phi, phi_noise, out):
    with ExitStack() as ctx:
        def sb(name, shape, dt=F32):
            return ctx.enter_context(nc.sbuf_tensor(name, shape, dt))

        def bank(name):
            return ctx.enter_context(nc.psum_tensor(name, [P, DIM], F32))

        def sem(name):
            return ctx.enter_context(nc.semaphore(name))

        wk = sb("wk", [P, CH, HID])
        wqT = sb("wqT", [P, CH, DIM])
        wv = sb("wv", [P, CH, HID])
        wo = sb("wo", [P, CH, DIM])
        ctx_t = sb("ctx_t", [P, CH, KK])
        mask8 = sb("mask8", [P, KK], U8)
        bias_q = sb("bias_q", [P, CH])
        bias_k = sb("bias_k", [P, CH])
        bias_v = sb("bias_v", [P, CH])
        bo_rows = sb("bo_rows", [KEYS, DIM])
        angle_w = [sb(f"angle_w{i}", [P, CH * DIM]) for i in range(2)]
        angle_n = [sb(f"angle_n{i}", [P, CH * DIM]) for i in range(2)]
        turns = sb("turns", [P, CH * DIM])

        ones_mean = sb("ones_mean", [P, P])
        bq_cols = sb("bq_cols", [P, CH, P])
        kT = sb("kT", [P, CH, KK])
        vT = sb("vT", [P, CH, KK])
        a_raw = sb("a_raw", [P, CH, KK])
        a_mid = sb("a_mid", [P, CH, KK])
        a_keys = sb("a_keys", [P, CH, KK])
        keep = sb("keep", [P, KK])
        keep_off = sb("keep_off", [P, KK])
        c_mid = sb("c_mid", [P, KK])
        c_keys = sb("c_keys", [P, KK])
        vw = sb("vw", [KEYS, BATCH, DIM])
        w_hi = [sb(f"w_hi{i}", [P, CH, DIM], F16) for i in range(2)]
        w_lo = [sb(f"w_lo{i}", [P, CH, DIM], F16) for i in range(2)]
        vw_scaled = sb("vw_scaled", [KEYS, BATCH, DIM])
        vw_lo = sb("vw_lo", [KEYS, BATCH, DIM], F16)
        vw_stack = [sb(f"vw_stack{i}", [P, BATCH, DIM], F16) for i in range(2)]
        ones_row = sb("ones_row", [1, P])
        key_max = sb("key_max", [KEYS, 1])
        vw_max = sb("vw_max", [1, 1])
        vw_max_all = sb("vw_max_all", [P, 1])
        vw_max_inv = sb("vw_max_inv", [P, 1])
        vw_scale = sb("vw_scale", [P, 1])
        total_scale = sb("total_scale", [P, 1])
        ident = sb("ident", [P, P])
        minus_half = sb("minus_half", [P, TILES])
        eps = sb("eps", [P, TILES])
        zero = sb("zero", [P, 1])

        xb = [sb(f"xb{i}", [P, TILES, DIM]) for i in range(2)]
        xTb = sb("xTb", [P, CH, ROWS])
        stats1 = sb("stats1", [P, TILES, 6])
        mv1 = sb("mv1", [P, TILES, 2])
        veps1 = sb("veps1", [P, TILES])
        rstd1 = sb("rstd1", [P, TILES])
        logits = sb("logits", [P, TILES, KEYS])
        shifted = sb("shifted", [P, TILES, KEYS])
        top = sb("top", [P, TILES])
        probs = sb("probs", [P, TILES, KEYS])
        total = sb("total", [P, TILES])
        inv_total = sb("inv_total", [P, TILES])
        probsT = sb("probsT", [KEYS, ROWS])
        p_split = sb("p_split", [P, TILES, 2 * P], F16)
        pT = sb("pT", [P, 2 * TILES, P], F16)
        scaled_total = sb("scaled_total", [P, TILES])
        x2 = [sb(f"x2_{i}", [P, TILES, DIM]) for i in range(2)]
        stats2 = sb("stats2", [P, TILES, 6])
        mv2 = sb("mv2", [P, TILES, 2])
        veps2 = sb("veps2", [P, TILES])
        rstd2 = sb("rstd2", [P, TILES])
        minus_mean2 = sb("minus_mean2", [P, TILES])
        shift2 = sb("shift2", [P, TILES])
        h = [sb(f"h{i}", [P, DIM]) for i in range(2)]
        h_split = [sb(f"h_split{j}", [P, 2, DIM], F16) for j in range(TILES)]
        hT = [sb(f"hT{j}", [P, 2, CH, P], F16) for j in range(TILES)]
        sq_re = [sb(f"sq_re{i}", [P, DIM]) for i in range(2)]
        sq_im = [sb(f"sq_im{i}", [P, DIM]) for i in range(2)]
        power = wk
        result = wv

        re_bank = [bank("re0"), bank("re1")]
        im_bank = [bank("im0"), bank("im1")]
        score_bank = bank("score_bank")
        pT_bank = bank("pT_bank")
        att_bank = [bank("att0"), bank("att1")]
        prep = [re_bank[0], re_bank[1], im_bank[0], im_bank[1], score_bank, pT_bank, att_bank[0], att_bank[1]]

        ld_ctx, ld_wq, ld_wv, ld_wo = (sem(f"ld_{n}") for n in ("ctx", "wq", "wv", "wo"))
        ld_wk = [sem(f"ld_wk{half}") for half in range(2)]
        ld_bq, ld_bk, ld_bv, ld_bo, ld_mask = (sem(f"ld_{n}") for n in ("bq", "bk", "bv", "bo", "mask"))
        ld_angle = [[sem(f"ld_{n}{half}") for half in range(2)] for n in ("theta", "phi")]
        consts_made = sem("consts_made")
        v_consts = sem("v_consts")
        kT_mm, kT_ready = sem("kT_mm"), sem("kT_ready")
        a_mm, a_copied = sem("a_mm"), sem("a_copied")
        c_mm, mean_mm = sem("c_mm"), sem("mean_mm")
        a_centred, keys_ready = sem("a_centred"), sem("keys_ready")
        vT_mm, vT_ready = sem("vT_mm"), sem("vT_ready")
        vw_mm, vw_ready = sem("vw_mm"), sem("vw_ready")
        vw_abs_made = sem("vw_abs_made")
        key_max_made, key_max_mm = sem("key_max_made"), sem("key_max_mm")
        vw_max_made, vw_max_mm, vw_max_read = sem("vw_max_made"), sem("vw_max_mm"), sem("vw_max_read")
        vw_scale_made, vw_scaled_made = sem("vw_scale_made"), sem("vw_scaled_made")
        vw_hi_ready, vw_lo_ready, vw_stacked = sem("vw_hi_ready"), sem("vw_lo_ready"), sem("vw_stacked")
        angle_summed = [sem("theta_summed"), sem("phi_summed")]
        turns_rounded, turns_made = sem("turns_rounded"), sem("turns_made")
        angle_step = sem("angle_step")
        angle_ready = sem("angle_ready")
        sine_made = sem("sine_made")
        w_hi_ready, w_ready = sem("w_hi_ready"), sem("w_ready")
        x_loaded = [sem("x_loaded0"), sem("x_loaded1")]
        xT_loaded, stored = sem("xT_loaded"), sem("stored")
        stats1_made, mean1_made, eps1_added, rstd1_made = (sem(f"{n}") for n in ("stats1_made", "mean1_made", "eps1_added", "rstd1_made"))
        scores_mm, scores_read, top_found, shifted_made = (sem(f"{n}") for n in ("scores_mm", "scores_read", "top_found", "shifted_made"))
        probs_made, total_made, inv_total_made = sem("probs_made"), sem("total_made"), sem("inv_total_made")
        pT_mm, pT_copied = sem("pT_mm"), sem("pT_copied")
        pad_made, p_hi_made, p_lo_made = sem("pad_made"), sem("p_hi_made"), sem("p_lo_made")
        pT_ready, total_scaled = sem("pT_ready"), sem("total_scaled")
        att_mm, x2_made = sem("att_mm"), sem("x2_made")
        stats2_made, mean2_made, eps2_added, rstd2_made = (sem(f"{n}") for n in ("stats2_made", "mean2_made", "eps2_added", "rstd2_made"))
        minus_mean2_made, shift2_made = sem("minus_mean2_made"), sem("shift2_made")
        h_made, hi_made, lo_made = sem("h_made"), sem("hi_made"), sem("lo_made")
        transposes_sent = sem("transposes_sent")
        hT_ready = [sem(f"hT_ready{j}") for j in range(TILES)]
        re_mm, im_mm, re_squared, im_squared, power_made = (sem(f"{n}") for n in ("re_mm", "im_mm", "re_squared", "im_squared", "power_made"))
        root_made, result_made = sem("root_made"), sem("result_made")

        LAST = GROUPS - 1

        block = ctx.enter_context(nc.Block())

        @block.sync
        def _(sp):
            def load_x(batch, blk):
                sp.dma_start(xb[batch][:, :, :], x[batch, blk]).then_inc(x_loaded[batch], 16)

            def load_xT(batch, blk):
                sp.dma_start(xTb[:, :, :], xT[batch, blk]).then_inc(xT_loaded, 16)

            def load_angles(part, half):
                cols_ = slice(HALF * half, HALF * half + HALF)
                w_dram, n_dram = ((theta, theta_noise), (phi, phi_noise))[part]
                sp.dma_start(angle_w[part][:, cols_], w_dram[:, cols_]).then_inc(ld_angle[part][half], 16)
                sp.dma_start(angle_n[part][:, cols_], n_dram[:, cols_]).then_inc(ld_angle[part][half], 16)

            sp.dma_start(ctx_t[:, :, :], ctxT).then_inc(ld_ctx, 16)
            for half in range(2):
                chunks = slice(CH // 2 * half, CH // 2 * half + CH // 2)
                sp.dma_start(wk[:, chunks, :], Wk[:, chunks, :]).then_inc(ld_wk[half], 16)
            sp.dma_start(wqT[:, :, :], WqT).then_inc(ld_wq, 16)
            load_angles(0, 0)
            load_angles(0, 1)
            sp.dma_start(wv[:, :, :], Wv).then_inc(ld_wv, 16)
            load_xT(0, 0)
            load_x(0, 0)
            sp.dma_start(wo[:, :, :], Wo).then_inc(ld_wo, 16)
            load_angles(1, 0)
            load_angles(1, 1)
            load_x(1, 0)
            sp.wait_ge(scores_mm, 1)
            load_xT(1, 0)

            def transpose_h(m, tiles):
                for j in tiles:
                    sp.wait_ge(lo_made, TILES * m + j + 1)
                    sp.sem_inc(transposes_sent, 1)
                    sp.dma_start_transpose(hT[j][:, :, :, :].rearrange("p s c r -> p (s c) r"),
                                           h_split[j][:, :, :].rearrange("p s d -> p (s d)")).then_inc(hT_ready[j], 16)

            def transpose_probs(m):
                sp.wait_ge(p_lo_made, m)
                sp.sem_inc(transposes_sent, 1)
                sp.dma_start_transpose(pT[:, :, :], p_split[:, :, :].rearrange("p t s -> p (t s)")).then_inc(pT_ready, 16)

            def step(n, batch, blk, load):
                if load:
                    sp.wait_ge(x2_made, TILES * (n + 1))
                    load_x(batch, blk)
                transpose_h(n, [2])
                if not isinstance(n, int) or n < LAST:
                    transpose_probs(n + 1)
                transpose_h(n, [3])
                if load:
                    sp.wait_ge(scores_mm, n + 2)
                    load_xT(batch, blk)
                sp.wait_ge(result_made, n)
                sp.dma_start(out[1 - batch, blk - 1 - (1 - batch)], result[:, :, :]).then_inc(stored, 16)
                if not isinstance(n, int) or n < LAST:
                    transpose_h(n + 1, [0, 1])

            transpose_h(0, [0, 1])
            sp.wait_ge(x2_made, TILES)
            load_x(0, 1)
            transpose_h(0, [2])
            sp.wait_ge(scores_mm, 2)
            load_xT(0, 1)
            transpose_h(0, [3])
            sp.wait_ge(vw_hi_ready, 1)
            sp.dma_start(vw_stack[1][REST - KEYS:REST, :, :],
                         vw_stack[0][0:KEYS, :, :]).then_inc(vw_stacked, 16)
            sp.wait_ge(vw_lo_ready, 1)
            sp.dma_start(vw_stack[0][KEYS:P, :, :], vw_lo[0:P - KEYS, :, :]).then_inc(vw_stacked, 16)
            sp.dma_start(vw_stack[1][0:REST - KEYS, :, :], vw_lo[P - KEYS:KEYS, :, :]).then_inc(vw_stacked, 16)
            transpose_probs(1)
            transpose_h(1, [0, 1])
            with sp.Fori(0, 2) as i:
                step(2 * i + 1, 1, i + 1, True)
                step(2 * i + 2, 0, i + 2, True)
            step(5, 1, 3, True)
            step(6, 0, 4, False)
            step(7, 1, 4, False)
            for j in range(TILES):
                sp.wait_ge(result_made, LAST + j + 1)
                sp.dma_start(out[1, BLOCKS - 1, :, j, :], result[:, j, :]).then_inc(stored, 16)
            sp.wait_ge(stored, 16 * (LAST + TILES))

        @block.gpsimd
        def _(pool):
            nc.gpsimd.memset(minus_half[:, :], -0.5)
            nc.gpsimd.memset(eps[:, :], LN_EPS)
            nc.gpsimd.memset(zero[:, :], 0.0)
            nc.gpsimd.memset(p_split[:, :, STACK:2 * P], 0.0).then_inc(pad_made, 1)
            nc.gpsimd.memset(ones_row[:, :], 1.0)
            nc.gpsimd.memset(ident[:, :], 0.0).then_inc(consts_made, 1)
            pool.wait_ge(consts_made, 1)
            nc.gpsimd.affine_select(out=ident[:, :], in_=ident[:, :], compare_op=ALU.not_equal, fill=1.0,
                                    base=0, pattern=[[-1, P]], channel_multiplier=1).then_inc(consts_made, 1)

            def sum_angle(half):
                pool.wait_ge(ld_angle[1][half], 32)
                cols_ = slice(HALF * half, HALF * half + HALF)
                nc.gpsimd.tensor_tensor(angle_w[1][:, cols_], angle_w[1][:, cols_], angle_n[1][:, cols_],
                                        ALU.add).then_inc(angle_summed[1], 1)

            def rstd_of_x(m):
                pool.wait_ge(mean1_made, m + 1)
                nc.gpsimd.tensor_tensor(veps1[:, :], mv1[:, :, 1], eps[:, :], ALU.add).then_inc(eps1_added, 1)
                pool.wait_ge(eps1_added, m + 1)
                nc.gpsimd.tensor_tensor(rstd1[:, :], veps1[:, :], minus_half[:, :], ALU.pow).then_inc(rstd1_made, 1)

            def rstd_of_x2(m, j):
                pool.wait_ge(mean2_made, TILES * m + j + 1)
                nc.gpsimd.tensor_tensor(veps2[:, j:j + 1], mv2[:, j, 1:2], eps[:, 0:1], ALU.add).then_inc(eps2_added, 1)
                nc.gpsimd.tensor_tensor(minus_mean2[:, j:j + 1], zero[:, :], mv2[:, j, 0:1],
                                        ALU.subtract).then_inc(minus_mean2_made, 1)
                pool.wait_ge(eps2_added, TILES * m + j + 1)
                nc.gpsimd.tensor_tensor(rstd2[:, j:j + 1], veps2[:, j:j + 1], minus_half[:, 0:1], ALU.pow).then_inc(rstd2_made, 1)
                pool.wait_ge(minus_mean2_made, TILES * m + j + 1)
                pool.wait_ge(rstd2_made, TILES * m + j + 1)
                nc.gpsimd.tensor_tensor(shift2[:, j:j + 1], minus_mean2[:, j:j + 1], rstd2[:, j:j + 1],
                                        ALU.mult).then_inc(shift2_made, 1)

            def step(m):
                rstd_of_x(m + 1)
                for j in range(TILES):
                    rstd_of_x2(m, j)

            rstd_of_x(0)
            sum_angle(0)
            sum_angle(1)
            for j in range(TILES):
                rstd_of_x2(0, j)
            rstd_of_x(1)
            pool.wait_ge(vw_hi_ready, 1)
            nc.gpsimd.tensor_tensor(vw_lo[:, :, :], vw_scaled[:, :, :], vw_stack[0][0:KEYS, :, :],
                                    ALU.subtract).then_inc(vw_lo_ready, 1)
            with pool.Fori(0, 3) as i:
                step(2 * i + 1)
                step(2 * i + 2)
            for j in range(TILES):
                rstd_of_x2(LAST, j)

        @block.tensor
        def _(pe):
            pe.wait_ge(ld_ctx, 16)
            pe.wait_ge(ld_wk[0], 16)
            for c in range(CH):
                for k in range(CH // 2):
                    nc.tensor.matmul(prep[c][:, 0:KK], wk[:, k, P * c:P * c + P], ctx_t[:, k, :],
                                     start=(k == 0), stop=False)
            pe.wait_ge(ld_wk[1], 16)
            for c in range(CH):
                for k in range(CH // 2, CH):
                    last = nc.tensor.matmul(prep[c][:, 0:KK], wk[:, k, P * c:P * c + P], ctx_t[:, k, :],
                                            start=False, stop=(k == CH - 1))
                last.then_inc(kT_mm, 1)
            pe.wait_ge(ld_wq, 16)
            pe.wait_ge(kT_ready, CH)
            for c in range(CH):
                for k in range(CH):
                    last = nc.tensor.matmul(prep[4 + c][:, 0:KK], wqT[:, k, P * c:P * c + P], kT[:, k, :],
                                            start=(k == 0), stop=(k == CH - 1))
                last.then_inc(a_mm, 1)
            pe.wait_ge(v_consts, 3)
            for k in range(CH):
                last = nc.tensor.matmul(prep[0][:, 0:KK], bq_cols[:, k, :], kT[:, k, :],
                                        start=(k == 0), stop=(k == CH - 1))
            last.then_inc(c_mm, 1)
            pe.wait_ge(a_copied, CH)
            for k in range(CH):
                last = nc.tensor.matmul(prep[1][:, 0:KK], ones_mean[:, :], a_raw[:, k, :],
                                        start=(k == 0), stop=(k == CH - 1))
            last.then_inc(mean_mm, 1)

            def scores(m, batch):
                pe.wait_ge(xT_loaded, 16 * (m + 1))
                if not isinstance(m, int) or m > 0:
                    pe.wait_ge(scores_read, m)
                for j in range(TILES):
                    for k in range(CH):
                        last = nc.tensor.matmul(score_bank[:, KEYS * j:KEYS * j + KEYS], xTb[:, k, P * j:P * j + P],
                                                a_keys[:, k, KEYS * batch:KEYS * batch + KEYS],
                                                start=(k == 0), stop=(k == CH - 1))
                last.then_inc(scores_mm, 1)

            def attend_first(j):
                if j >= 2:
                    pe.wait_ge(x2_made, j - 1)
                nc.tensor.matmul(att_bank[j % 2][:, :], probsT[:, P * j:P * j + P], vw[:, 0, :],
                                 start=True, stop=True).then_inc(att_mm, 1)

            def attend(m, batch, j):
                pe.wait_ge(pT_ready, 16 * m)
                pe.wait_ge(x2_made, TILES * m + j - 1)
                nc.tensor.matmul(att_bank[j % 2][:, :], pT[:, 2 * j, :], vw_stack[0][:, batch, :],
                                 start=True, stop=False)
                nc.tensor.matmul(att_bank[j % 2][:, :], pT[0:REST, 2 * j + 1, :], vw_stack[1][0:REST, batch, :],
                                 start=False, stop=True).then_inc(att_mm, 1)

            def feed(n, j, part):
                bank_ = (re_bank, im_bank)[part][j % 2]
                pe.wait_ge(hT_ready[j], 16 * (n + 1))
                if j >= 2 or not isinstance(n, int) or n > 0:
                    pe.wait_ge((re_squared, im_squared)[part], TILES * n + j - 1)
                for k in range(CH):
                    nc.tensor.matmul(bank_[:, :], hT[j][:, 0, k, :], w_hi[part][:, k, :], start=(k == 0), stop=False)
                    nc.tensor.matmul(bank_[:, :], hT[j][:, 0, k, :], w_lo[part][:, k, :], start=False, stop=False)
                    last = nc.tensor.matmul(bank_[:, :], hT[j][:, 1, k, :], w_hi[part][:, k, :],
                                            start=False, stop=(k == CH - 1))
                last.then_inc((re_mm, im_mm)[part], 1)

            def project_values(b):
                for k in range(CH):
                    last = nc.tensor.matmul(prep[b][0:KEYS, :], vT[:, k, KEYS * b:KEYS * b + KEYS], wo[:, k, :],
                                            start=(k == 0), stop=(k == CH - 1))
                last.then_inc(vw_mm, 1)

            pe.wait_ge(ld_wv, 16)
            for c in range(CH):
                bank_ = prep[2 + c] if c < 2 else prep[3 + c]
                for k in range(CH):
                    last = nc.tensor.matmul(bank_[:, 0:KK], wv[:, k, P * c:P * c + P], ctx_t[:, k, :],
                                            start=(k == 0), stop=(k == CH - 1))
                last.then_inc(vT_mm, 1)
            pe.wait_ge(keys_ready, 2)
            scores(0, 0)
            pe.wait_ge(ld_wo, 16)
            pe.wait_ge(vT_ready, CH)
            project_values(0)
            pe.wait_ge(consts_made, 2)
            pe.wait_ge(probs_made, 1)
            for j in range(TILES):
                last = nc.tensor.transpose(pT_bank[0:KEYS, P * j:P * j + P], probs[:, j, :], ident[:, :])
            last.then_inc(pT_mm, 1)
            pe.wait_ge(vw_ready, 1)
            pe.wait_ge(pT_copied, 1)
            attend_first(0)
            attend_first(1)
            project_values(1)
            attend_first(2)
            attend_first(3)
            scores(1, 1)

            def step(n, batch, more=True):
                feed(n, 0, 0)
                feed(n, 0, 1)
                feed(n, 1, 0)
                feed(n, 1, 1)
                attend(n + 1, batch, 0)
                feed(n, 2, 0)
                attend(n + 1, batch, 1)
                feed(n, 2, 1)
                attend(n + 1, batch, 2)
                feed(n, 3, 0)
                attend(n + 1, batch, 3)
                if more:
                    scores(n + 2, 1 - batch)
                feed(n, 3, 1)

            pe.wait_ge(w_ready, 2)
            feed(0, 0, 0)
            feed(0, 1, 0)
            pe.wait_ge(key_max_made, 1)
            nc.tensor.transpose(pT_bank[0:1, 0:KEYS], key_max[:, :], ident[0:KEYS, 0:KEYS]).then_inc(key_max_mm, 1)
            pe.wait_ge(vw_max_made, 1)
            nc.tensor.matmul(pT_bank[:, P:P + 1], ones_row[:, :], vw_max[:, :], start=True, stop=True).then_inc(vw_max_mm, 1)
            pe.wait_ge(w_ready, 4)
            feed(0, 0, 1)
            feed(0, 1, 1)
            feed(0, 2, 0)
            feed(0, 2, 1)
            scores(2, 0)
            pe.wait_ge(vw_stacked, 3 * 16)
            attend(1, 1, 0)
            feed(0, 3, 0)
            attend(1, 1, 1)
            attend(1, 1, 2)
            feed(0, 3, 1)
            attend(1, 1, 3)
            with pe.Fori(0, 2) as i:
                step(2 * i + 1, 0)
                step(2 * i + 2, 1)
            step(5, 0)
            step(6, 1, False)
            for j in range(TILES):
                feed(LAST, j, 0)
                feed(LAST, j, 1)

        @block.scalar
        def _(act):
            act.dma_start(bias_k[:, :], bk).then_inc(ld_bk, 16)
            act.dma_start(bias_q[:, :], bq).then_inc(ld_bq, 16)
            act.dma_start(mask8[:, :], mask).then_inc(ld_mask, 16)
            act.dma_start(bias_v[:, :], bv).then_inc(ld_bv, 16)
            act.dma_start(bo_rows[:, :], bo).then_inc(ld_bo, 16)
            act.wait_ge(ld_bk, 16)
            for c in range(CH):
                act.wait_ge(kT_mm, c + 1)
                nc.scalar.activation(kT[:, c, :], prep[c][:, 0:KK], ACT.Identity,
                                     bias=bias_k[:, c:c + 1]).then_inc(kT_ready, 1)
            def turns_of(part, half):
                u = 2 * part + half
                act.wait_ge(angle_summed[part], half + 1)
                if part:
                    act.wait_ge(angle_step, 2 * half + 2)
                cols_ = slice(HALF * half, HALF * half + HALF)
                nc.scalar.activation(turns[:, cols_], angle_w[part][:, cols_], ACT.Copy,
                                     bias=ROUND, scale=1.0 / (2.0 * math.pi)).then_inc(turns_rounded, 1)
                act.wait_ge(turns_rounded, u + 1)
                nc.scalar.activation(turns[:, cols_], turns[:, cols_], ACT.Copy, bias=-ROUND).then_inc(turns_made, 1)

            def sine(part, half):
                u = 2 * part + half
                act.wait_ge(angle_ready, u + 1)
                cols_ = slice(HALF * half, HALF * half + HALF)
                nc.scalar.activation(angle_n[part][:, cols_], angle_w[part][:, cols_], ACT.Sin).then_inc(sine_made, 1)
                act.wait_ge(sine_made, u + 1)
                nc.scalar.activation(w_hi[part][:, :, :].rearrange("p c d -> p (c d)")[:, cols_], angle_n[part][:, cols_],
                                     ACT.Copy, scale=W_SCALE).then_inc(w_hi_ready, 1)

            def exps(m):
                act.wait_ge(shifted_made, m + 1)
                nc.scalar.activation(probs[:, :, :], shifted[:, :, :], ACT.Exp).then_inc(probs_made, 1)

            def high_probs(m):
                act.wait_ge(probs_made, m + 1)
                if not isinstance(m, int) or m > 1:
                    act.wait_ge(pT_ready, 16 * (m - 1))
                nc.scalar.activation(p_split[:, :, 0:2 * KEYS].rearrange("p t (s k) -> p t s k", s=2),
                                     probs[:, :, :].unsqueeze(2).to_broadcast([P, TILES, 2, KEYS]),
                                     ACT.Copy, scale=P_SCALE).then_inc(p_hi_made, 1)

            def high_half(m, b, j):
                if j >= 2 or not isinstance(m, int) or m > 0:
                    act.wait_ge(lo_made, TILES * m + j - 1)
                act.wait_ge(shift2_made, TILES * m + j + 1)
                nc.scalar.activation(h[j % 2][:, :], x2[b][:, j, :], ACT.Identity,
                                     bias=shift2[:, j:j + 1], scale=rstd2[:, j:j + 1]).then_inc(h_made, 1)
                act.wait_ge(h_made, TILES * m + j + 1)
                if not isinstance(m, int) or m > 0:
                    act.wait_ge(hT_ready[j], 16 * m)
                nc.scalar.activation(h_split[j][:, 0, :], h[j % 2][:, :], ACT.Copy, scale=H_SCALE).then_inc(hi_made, 1)

            def square(n, j, part):
                act.wait_ge((re_mm, im_mm)[part], TILES * n + j + 1)
                if j >= 2 or not isinstance(n, int) or n > 0:
                    act.wait_ge(power_made, TILES * n + j - 1)
                nc.scalar.activation((sq_re, sq_im)[part][j % 2][:, :], (re_bank, im_bank)[part][j % 2][:, :],
                                     ACT.Square, scale=UNSCALE).then_inc((re_squared, im_squared)[part], 1)

            def roots(n):
                act.wait_ge(power_made, TILES * (n + 1))
                nc.scalar.activation(power[:, :, :], power[:, :, :], ACT.Sqrt).then_inc(root_made, 1)

            for c in range(CH):
                act.wait_ge(a_mm, c + 1)
                nc.scalar.activation(a_raw[:, c, :], prep[4 + c][:, 0:KK], ACT.Copy, scale=SM_SCALE).then_inc(a_copied, 1)
            turns_of(0, 0)
            turns_of(0, 1)
            act.wait_ge(ld_bv, 16)
            for c in range(CH):
                bank_ = prep[2 + c] if c < 2 else prep[3 + c]
                act.wait_ge(vT_mm, c + 1)
                nc.scalar.activation(vT[:, c, :], bank_[:, 0:KK], ACT.Identity,
                                     bias=bias_v[:, c:c + 1]).then_inc(vT_ready, 1)
            sine(0, 0)
            exps(0)
            act.wait_ge(pT_mm, 1)
            nc.scalar.activation(probsT[:, :], pT_bank[0:KEYS, :], ACT.Copy).then_inc(pT_copied, 1)
            turns_of(1, 0)
            sine(0, 1)
            high_half(0, 0, 0)
            turns_of(1, 1)
            high_half(0, 0, 1)
            act.wait_ge(vw_ready, 2)
            nc.scalar.activation(vw_scaled[:, :, :], vw[:, :, :], ACT.Abs).then_inc(vw_abs_made, 1)
            sine(1, 0)
            high_half(0, 0, 2)
            sine(1, 1)
            high_half(0, 0, 3)
            square(0, 0, 0)
            square(0, 1, 0)
            square(0, 0, 1)
            act.wait_ge(vw_scale_made, 2)
            nc.scalar.activation(vw_scaled[:, :, :], vw[:, :, :], ACT.Copy,
                                 scale=vw_scale[0:KEYS, 0:1]).then_inc(vw_scaled_made, 1)
            act.wait_ge(vw_scaled_made, 1)
            nc.scalar.activation(vw_stack[0][0:KEYS, :, :], vw_scaled[:, :, :], ACT.Copy).then_inc(vw_hi_ready, 1)
            exps(1)
            high_probs(1)
            square(0, 1, 1)
            square(0, 2, 0)
            square(0, 2, 1)
            high_half(1, 1, 0)
            high_half(1, 1, 1)
            square(0, 3, 0)
            high_half(1, 1, 2)

            def step(n, b):
                exps(n + 1)
                high_probs(n + 1)
                square(n - 1, 3, 1)
                high_half(n, b, 3)
                square(n, 0, 0)
                square(n, 0, 1)
                roots(n - 1)
                square(n, 1, 0)
                square(n, 1, 1)
                square(n, 2, 0)
                high_half(n + 1, 1 - b, 0)
                square(n, 2, 1)
                high_half(n + 1, 1 - b, 1)
                square(n, 3, 0)
                high_half(n + 1, 1 - b, 2)

            with act.Fori(0, 3) as i:
                step(2 * i + 1, 1)
                step(2 * i + 2, 0)
            square(LAST - 1, 3, 1)
            high_half(LAST, 1, 3)
            roots(LAST - 1)
            for j in range(TILES):
                square(LAST, j, 0)
                square(LAST, j, 1)
                act.wait_ge(power_made, TILES * LAST + j + 1)
                nc.scalar.activation(power[:, j, :], power[:, j, :], ACT.Sqrt).then_inc(root_made, 1)

        @block.vector
        def _(dve):
            nc.vector.memset(ones_mean[:, :], 1.0 / DIM).then_inc(v_consts, 1)
            nc.vector.memset(bq_cols[:, :, :], SM_SCALE).then_inc(v_consts, 1)
            dve.wait_ge(ld_bq, 16)
            dve.wait_ge(v_consts, 2)
            nc.vector.tensor_tensor(bq_cols[:, :, :], bq_cols[:, :, :],
                                    bias_q[:, :].unsqueeze(2).to_broadcast([P, CH, P]), ALU.mult).then_inc(v_consts, 1)
            dve.wait_ge(ld_mask, 16)
            nc.vector.tensor_copy(keep[:, :], mask8[:, :]).then_inc(v_consts, 1)
            dve.wait_ge(v_consts, 4)
            nc.vector.tensor_scalar(keep_off[:, :], keep[:, :], MASKED, -MASKED, ALU.mult, ALU.add).then_inc(v_consts, 1)

            def sum_angle(half):
                dve.wait_ge(ld_angle[0][half], 32)
                cols_ = slice(HALF * half, HALF * half + HALF)
                nc.vector.scalar_tensor_tensor(out=angle_w[0][:, cols_], in0=angle_w[0][:, cols_], scalar=0.5 * math.pi,
                                               in1=angle_n[0][:, cols_], op0=ALU.add,
                                               op1=ALU.add).then_inc(angle_summed[0], 1)

            def reduce_angle(part, half):
                u = 2 * part + half
                w = angle_w[part][:, HALF * half:HALF * half + HALF]
                k = turns[:, HALF * half:HALF * half + HALF]
                dve.wait_ge(turns_made, u + 1)
                nc.vector.scalar_tensor_tensor(out=w, in0=k, scalar=-TURN_HI, in1=w,
                                               op0=ALU.mult, op1=ALU.add).then_inc(angle_step, 1)
                dve.wait_ge(angle_step, 2 * u + 1)
                nc.vector.scalar_tensor_tensor(out=w, in0=k, scalar=-TURN_LO, in1=w,
                                               op0=ALU.mult, op1=ALU.add).then_inc(angle_step, 1)
                dve.wait_ge(angle_step, 2 * u + 2)
                nc.vector.tensor_scalar(w, w, SIN_MAX, -SIN_MAX, ALU.min, ALU.max).then_inc(angle_ready, 1)

            def low_half_of_sine(part, half):
                dve.wait_ge(w_hi_ready, 2 * part + half + 1)
                cols_ = slice(HALF * half, HALF * half + HALF)
                nc.vector.scalar_tensor_tensor(
                    out=w_lo[part][:, :, :].rearrange("p c d -> p (c d)")[:, cols_], in0=angle_n[part][:, cols_],
                    scalar=W_SCALE, in1=w_hi[part][:, :, :].rearrange("p c d -> p (c d)")[:, cols_],
                    op0=ALU.mult, op1=ALU.subtract).then_inc(w_ready, 1)

            def stats_of_x(b, blk):
                dve.wait_ge(x_loaded[b], 16 * (blk + 1))
                for j in range(TILES):
                    last = nc.vector.bn_stats(stats1[:, j, :], xb[b][:, j, :])
                last.then_inc(stats1_made, 1)

            def mean_of_x(m):
                for j in range(TILES):
                    last = nc.vector.bn_aggr(mv1[:, j, :], stats1[:, j, :])
                last.then_inc(mean1_made, 1)

            def softmax_shift(m, b):
                dve.wait_ge(scores_mm, m + 1)
                dve.wait_ge(rstd1_made, m + 1)
                if not isinstance(m, int) or m > 0:
                    dve.wait_ge(shifted_made, m)
                for j in range(TILES):
                    last = nc.vector.scalar_tensor_tensor(
                        out=logits[:, j, :], in0=score_bank[:, KEYS * j:KEYS * j + KEYS], scalar=rstd1[:, j:j + 1],
                        in1=c_keys[:, KEYS * b:KEYS * b + KEYS], op0=ALU.mult, op1=ALU.add)
                last.then_inc(scores_read, 1)
                dve.wait_ge(scores_read, m + 1)
                nc.vector.tensor_reduce(top[:, :], logits[:, :, :], AX.X, ALU.max).then_inc(top_found, 1)
                dve.wait_ge(top_found, m + 1)
                if not isinstance(m, int) or m > 0:
                    dve.wait_ge(probs_made, m)
                nc.vector.tensor_tensor(shifted[:, :, :], logits[:, :, :],
                                        top[:, :].unsqueeze(2).to_broadcast([P, TILES, KEYS]),
                                        ALU.subtract).then_inc(shifted_made, 1)

            def softmax_total(m):
                dve.wait_ge(probs_made, m + 1)
                if not isinstance(m, int) or m > 0:
                    dve.wait_ge(inv_total_made, m)
                nc.vector.tensor_reduce(total[:, :], probs[:, :, :], AX.X, ALU.add).then_inc(total_made, 1)
                dve.wait_ge(total_made, m + 1)
                if not isinstance(m, int) or m > 0:
                    nc.vector.tensor_scalar(scaled_total[:, :], total[:, :], total_scale[:, 0:1], None,
                                            ALU.mult).then_inc(total_scaled, 1)
                    dve.wait_ge(total_scaled, m)
                    dve.wait_ge(x2_made, TILES * m)
                    nc.vector.reciprocal(inv_total[:, :], scaled_total[:, :]).then_inc(inv_total_made, 1)
                else:
                    nc.vector.reciprocal(inv_total[:, :], total[:, :]).then_inc(inv_total_made, 1)

            def low_probs(m):
                dve.wait_ge(p_hi_made, m)
                nc.vector.scalar_tensor_tensor(out=p_split[:, :, 2 * KEYS:STACK], in0=probs[:, :, :], scalar=P_SCALE,
                                               in1=p_split[:, :, 0:KEYS], op0=ALU.mult,
                                               op1=ALU.subtract).then_inc(p_lo_made, 1)

            def residual(m, b, j):
                dve.wait_ge(att_mm, TILES * m + j + 1)
                dve.wait_ge(inv_total_made, m + 1)
                if not isinstance(m, int) or m > 1:
                    dve.wait_ge(result_made, m - 1)
                nc.vector.scalar_tensor_tensor(out=x2[b][:, j, :], in0=att_bank[j % 2][:, :], scalar=inv_total[:, j:j + 1],
                                               in1=xb[b][:, j, :], op0=ALU.mult, op1=ALU.add).then_inc(x2_made, 1)
                dve.wait_ge(x2_made, TILES * m + j + 1)
                nc.vector.bn_stats(stats2[:, j, :], x2[b][:, j, :]).then_inc(stats2_made, 1)

            def stats_ready(m, j):
                dve.wait_ge(stats2_made, TILES * m + j + 1)

            def mean_of_x2(m, j):
                nc.vector.bn_aggr(mv2[:, j, :], stats2[:, j, :]).then_inc(mean2_made, 1)

            def low_half(m, j):
                dve.wait_ge(hi_made, TILES * m + j + 1)
                nc.vector.scalar_tensor_tensor(out=h_split[j][:, 1, :], in0=h[j % 2][:, :],
                                               scalar=H_SCALE, in1=h_split[j][:, 0, :],
                                               op0=ALU.mult, op1=ALU.subtract).then_inc(lo_made, 1)

            def add_squares(n, j):
                dve.wait_ge(re_squared, TILES * n + j + 1)
                dve.wait_ge(im_squared, TILES * n + j + 1)
                if not isinstance(n, int) or n > 0:
                    dve.wait_ge(result_made, n)
                nc.vector.tensor_tensor(power[:, j, :], sq_re[j % 2][:, :], sq_im[j % 2][:, :],
                                        ALU.add).then_inc(power_made, 1)

            def finish(n, b):
                dve.wait_ge(root_made, n + 1)
                if not isinstance(n, int) or n > 0:
                    dve.wait_ge(stored, 16 * n)
                nc.vector.tensor_tensor(result[:, :, :], x2[b][:, :, :], power[:, :, :], ALU.add).then_inc(result_made, 1)

            sum_angle(0)
            sum_angle(1)
            dve.wait_ge(mean_mm, 1)
            nc.vector.tensor_tensor(a_mid[:, :, :], a_raw[:, :, :],
                                    prep[1][:, 0:KK].unsqueeze(1).to_broadcast([P, CH, KK]),
                                    ALU.subtract).then_inc(a_centred, 1)
            dve.wait_ge(c_mm, 1)
            nc.vector.tensor_tensor(c_mid[:, :], prep[0][:, 0:KK], keep[:, :], ALU.mult).then_inc(a_centred, 1)
            dve.wait_ge(a_centred, 2)
            nc.vector.tensor_tensor(a_keys[:, :, :], a_mid[:, :, :],
                                    keep[:, :].unsqueeze(1).to_broadcast([P, CH, KK]), ALU.mult).then_inc(keys_ready, 1)
            dve.wait_ge(v_consts, 5)
            nc.vector.tensor_tensor(c_keys[:, :], c_mid[:, :], keep_off[:, :], ALU.add).then_inc(keys_ready, 1)
            def values_ready(b):
                dve.wait_ge(vw_mm, b + 1)
                nc.vector.tensor_tensor(vw[:, b, :], prep[b][0:KEYS, :], bo_rows[:, :], ALU.add).then_inc(vw_ready, 1)

            reduce_angle(0, 0)
            stats_of_x(0, 0)
            dve.wait_ge(stats1_made, 1)
            mean_of_x(0)
            low_half_of_sine(0, 0)
            softmax_shift(0, 0)
            dve.wait_ge(ld_bo, 16)
            values_ready(0)
            reduce_angle(0, 1)
            softmax_total(0)
            residual(0, 0, 0)
            stats_ready(0, 0)
            mean_of_x2(0, 0)
            residual(0, 0, 1)
            stats_ready(0, 1)
            mean_of_x2(0, 1)
            reduce_angle(1, 0)
            low_half(0, 0)
            low_half_of_sine(0, 1)
            residual(0, 0, 2)
            stats_ready(0, 2)
            mean_of_x2(0, 2)
            values_ready(1)
            low_half(0, 1)
            reduce_angle(1, 1)
            residual(0, 0, 3)
            stats_ready(0, 3)
            mean_of_x2(0, 3)
            low_half_of_sine(1, 0)
            dve.wait_ge(vw_abs_made, 1)
            nc.vector.tensor_reduce(key_max[:, :], vw_scaled[:, :, :].rearrange("p b d -> p (b d)"), AX.X,
                                    ALU.max).then_inc(key_max_made, 1)
            low_half(0, 2)
            dve.wait_ge(key_max_mm, 1)
            nc.vector.tensor_reduce(vw_max[:, :], pT_bank[0:1, 0:KEYS], AX.X, ALU.max).then_inc(vw_max_made, 1)
            low_half_of_sine(1, 1)
            low_half(0, 3)
            stats_of_x(1, 0)
            dve.wait_ge(vw_max_mm, 1)
            nc.vector.tensor_scalar(vw_max_all[:, :], pT_bank[:, P:P + 1], TINY, None, ALU.max).then_inc(vw_max_read, 1)
            dve.wait_ge(stats1_made, 2)
            mean_of_x(1)
            dve.wait_ge(vw_max_read, 1)
            nc.vector.reciprocal(vw_max_inv[:, :], vw_max_all[:, :]).then_inc(vw_max_read, 1)
            dve.wait_ge(vw_max_read, 2)
            nc.vector.tensor_scalar(vw_scale[:, :], vw_max_inv[:, :], V_SCALE, None, ALU.mult).then_inc(vw_scale_made, 1)
            nc.vector.tensor_scalar(total_scale[:, :], vw_max_inv[:, :], V_SCALE * P_SCALE, None,
                                    ALU.mult).then_inc(vw_scale_made, 1)
            softmax_shift(1, 1)
            add_squares(0, 0)
            low_probs(1)
            dve.wait_ge(vw_scale_made, 2)
            softmax_total(1)
            add_squares(0, 1)
            stats_of_x(0, 1)
            dve.wait_ge(stats1_made, 3)
            mean_of_x(2)
            residual(1, 1, 0)
            stats_ready(1, 0)
            mean_of_x2(1, 0)
            add_squares(0, 2)
            residual(1, 1, 1)
            stats_ready(1, 1)
            mean_of_x2(1, 1)
            low_half(1, 0)
            residual(1, 1, 2)
            stats_ready(1, 2)
            mean_of_x2(1, 2)
            low_half(1, 1)
            residual(1, 1, 3)
            stats_ready(1, 3)
            mean_of_x2(1, 3)
            low_half(1, 2)

            def step(n, b, blk):
                m, a = n + 1, 1 - b
                softmax_shift(m, a)
                low_probs(m)
                softmax_total(m)
                add_squares(n - 1, 3)
                low_half(n, 3)
                if blk is not None:
                    stats_of_x(b, blk)
                    dve.wait_ge(stats1_made, m + 2)
                finish(n - 1, a)
                if blk is not None:
                    mean_of_x(m + 1)
                add_squares(n, 0)
                residual(m, a, 0)
                stats_ready(m, 0)
                add_squares(n, 1)
                mean_of_x2(m, 0)
                residual(m, a, 1)
                stats_ready(m, 1)
                low_half(m, 0)
                mean_of_x2(m, 1)
                residual(m, a, 2)
                stats_ready(m, 2)
                add_squares(n, 2)
                mean_of_x2(m, 2)
                low_half(m, 1)
                residual(m, a, 3)
                stats_ready(m, 3)
                low_half(m, 2)
                mean_of_x2(m, 3)

            with dve.Fori(0, 2) as i:
                step(2 * i + 1, 1, i + 1)
                step(2 * i + 2, 0, i + 2)
            step(5, 1, 3)
            step(6, 0, None)
            add_squares(LAST - 1, 3)
            low_half(LAST, 3)
            finish(LAST - 1, 0)
            for j in range(TILES):
                add_squares(LAST, j)
                dve.wait_ge(root_made, LAST + j + 1)
                dve.wait_ge(stored, 16 * LAST)
                nc.vector.tensor_tensor(result[:, j, :], x2[1][:, j, :], power[:, j, :], ALU.add).then_inc(result_made, 1)


def kernel(x, ctx_1024, mask_BxS2_bk0, L0_xattn_Wq, L0_xattn_bq, L0_xattn_Wk, L0_xattn_bk, L0_xattn_Wv, L0_xattn_bv,
           L0_xattn_Wo, L0_xattn_bo, L0_ffn_theta, L0_ffn_phi, L0_ffn_theta_noise, L0_ffn_phi_noise):
    import concourse.bacc as bacc
    from concourse.bass_utils import run_bass_kernel_spmd

    def cols(w):
        w = np.asarray(w)
        return np.ascontiguousarray(w.reshape(CH, P, -1).transpose(1, 0, 2))

    rows = np.asarray(x).reshape(BATCH, BLOCKS, TILES, P, DIM)
    arrays = {
        "x": np.ascontiguousarray(rows.transpose(0, 1, 3, 2, 4)),
        "xT": np.ascontiguousarray(np.asarray(x).reshape(BATCH, BLOCKS, ROWS, CH, P).transpose(0, 1, 4, 3, 2)),
        "ctxT": cols(np.asarray(ctx_1024).reshape(KK, DIM).T),
        "mask": np.ascontiguousarray(np.broadcast_to(np.asarray(mask_BxS2_bk0).reshape(1, KK), (P, KK))),
        "Wk": cols(L0_xattn_Wk),
        "WqT": cols(np.asarray(L0_xattn_Wq).T),
        "Wv": cols(L0_xattn_Wv),
        "Wo": cols(L0_xattn_Wo),
        "bq": np.ascontiguousarray(np.asarray(L0_xattn_bq).reshape(CH, P).T),
        "bk": np.ascontiguousarray(np.asarray(L0_xattn_bk).reshape(CH, P).T),
        "bv": np.ascontiguousarray(np.asarray(L0_xattn_bv).reshape(CH, P).T),
        "bo": np.ascontiguousarray(np.broadcast_to(np.asarray(L0_xattn_bo).reshape(1, DIM), (KEYS, DIM))),
        "theta": cols(L0_ffn_theta).reshape(P, CH * DIM),
        "theta_noise": cols(L0_ffn_theta_noise).reshape(P, CH * DIM),
        "phi": cols(L0_ffn_phi).reshape(P, CH * DIM),
        "phi_noise": cols(L0_ffn_phi_noise).reshape(P, CH * DIM),
    }
    nc = bacc.Bacc("TRN2", target_bir_lowering=False, num_devices=1)
    args = {k: nc.dram_tensor(f"in_{k}", a.shape, mybir.dt.from_np(a.dtype), kind="ExternalInput").ap()
            for k, a in arrays.items()}
    out = nc.dram_tensor("out_rows", (BATCH, BLOCKS, P, TILES, DIM), F32, kind="ExternalOutput").ap()
    build(nc, **args, out=out)
    r = run_bass_kernel_spmd(nc, [{f"in_{k}": a for k, a in arrays.items()}], core_ids=[0])
    got = np.asarray(r.results[0]["out_rows"])
    return np.ascontiguousarray(got.transpose(0, 1, 3, 2, 4)).reshape(BATCH, SEQ, DIM)
```
